# Optimizing a Trainium2 kernel written in Bass

```python
import numpy as np
import jax
import jax.numpy as jnp

def _softmax(x, axis=-1):
    return jax.nn.softmax(x, axis=axis)

def _gelu(x):
    return jax.nn.gelu(x, approximate=True)

def _silu(x):
    return jax.nn.silu(x)

def _sigmoid(x):
    return jax.nn.sigmoid(x)

def _layernorm(x, axis=-1, eps=1e-05):
    m = jnp.mean(x, axis=axis, keepdims=True)
    v = jnp.var(x, axis=axis, keepdims=True)
    return (x - m) / jnp.sqrt(v + eps)

def _scatter_add(tgt, idx, src, axis=0):
    return tgt.at[idx].add(src)

def _segment_sum(src, seg, n):
    return jax.ops.segment_sum(src, seg, n)
kernel_name = 'mk_adj_preln_d4_adj_r2_19f644'

def setup_inputs(seed: int=0):
    np.random.seed(seed)
    _w = jnp.asarray

    def _rec_inputs():
        import jax
        import jax.numpy as jnp
        _gk = jax.random.key(seed)
        x = -0.0005146 + 1 * jax.random.normal(jax.random.fold_in(_gk, 1), (8, 1024, 128), jnp.float32)
        _w = (1.0 + jnp.arange(1024, dtype=jnp.float32)) ** (-0.5)
        _w = _w / _w.mean()
        _pij = jnp.clip(0.00390625 * _w[:, None] * _w[None, :], 0.0, 1.0)
        _a = jax.random.uniform(jax.random.fold_in(_gk, 2), (8, 1024, 1024)) < _pij
        adj = _a.astype(jnp.int32)
        return (x, adj)
    x, adj = _rec_inputs()

    def _L0_gnn_setup():
        import jax, jax.numpy as jnp
        import numpy as np
        B, N, C, OUT, S = (4, 1024, 128, 128, 25)
        DENSITY = 0.008
        key = jax.random.key(seed)
        kA, kX, kW = jax.random.split(key, 3)
        A = jax.random.bernoulli(kA, DENSITY, (B, N, N)).astype(jnp.int32)
        X = jax.random.normal(kX, (B, N, C), dtype=jnp.float32)
        W = jax.random.normal(kW, (2 * C, OUT), dtype=jnp.float32) * np.float32(1.0 / np.sqrt(2 * C))
        b = jnp.zeros((OUT,), dtype=jnp.float32)
        return {'A': A, 'X': X, 'W': W, 'b': b}
    _L0_gnn_all = _L0_gnn_setup()
    _L0_gnn_in = {k: v for k, v in _L0_gnn_all.items() if k in ('W', 'b')}
    del _L0_gnn_all

    def _L1_gnn_setup():
        import jax, jax.numpy as jnp
        import numpy as np
        B, N, F_IN, F_OUT = (8, 1024, 128, 128)
        key = jax.random.key(seed)
        k1, k2, k3, k4 = jax.random.split(key, 4)
        inp = jax.random.normal(k1, (B, N, F_IN), dtype=jnp.float32)
        adj = jax.random.randint(k2, (B, N, N), 0, 2, dtype=jnp.int32)
        W = jax.random.normal(k3, (F_IN, F_OUT), dtype=jnp.float32) * (1.414 * (6.0 / (F_IN + F_OUT)) ** 0.5)
        a = jax.random.normal(k4, (2 * F_OUT, 1), dtype=jnp.float32) * (1.414 * (6.0 / (2 * F_OUT + 1)) ** 0.5)
        return {'inp': inp, 'adj': adj, 'W': W, 'a': a}
    _L1_gnn_all = _L1_gnn_setup()
    _L1_gnn_in = {k: v for k, v in _L1_gnn_all.items() if k in ('W', 'a')}
    del _L1_gnn_all

    def _L2_gnn_setup():
        import jax, jax.numpy as jnp
        import numpy as np
        B, N, FIN, FOUT, H = (4, 512, 128, 128, 8)
        HID = FOUT // H
        ALPHA = 0.2
        NEG = -10000000000.0
        key = jax.random.key(seed)
        k1, k2, k3, k4, k5 = jax.random.split(key, 5)
        h = jax.random.normal(k1, (B, N, FIN), dtype=jnp.float32)
        adj = jax.random.randint(k2, (B, N, N), 0, 2, dtype=jnp.int32)
        W = jax.random.normal(k3, (FIN, H * HID), dtype=jnp.float32) * 0.05
        a = jax.random.normal(k4, (2 * HID,), dtype=jnp.float32) * 0.05
        bias = jax.random.normal(k5, (FOUT,), dtype=jnp.float32) * 0.05
        return {'h': h, 'adj': adj, 'W': W, 'a': a, 'bias': bias}
    _L2_gnn_all = _L2_gnn_setup()
    _L2_gnn_in = {k: v for k, v in _L2_gnn_all.items() if k in ('W', 'a', 'bias')}
    del _L2_gnn_all

    def _L3_gnn_setup():
        import jax, jax.numpy as jnp
        import numpy as np
        LEAKY_SLOPE = 0.2
        NEG_INF = -9000000000000000.0

        def _edge_scores(h, a_k):
            e = jnp.einsum('bid,bjd->bij', h * a_k[:, 0], h)
            return jax.nn.leaky_relu(e, negative_slope=LEAKY_SLOPE)
        key = jax.random.key(seed)
        k1, k2, k3, k4, k5, k6 = jax.random.split(key, 6)
        B, N, D = (32, 256, 128)
        hidden = jax.random.normal(k1, (B, N, D), dtype=jnp.float32)
        adj = jax.random.randint(k2, (B, N, N), 0, 5, dtype=jnp.int32)
        a_0 = jax.random.normal(k3, (D, 1), dtype=jnp.float32)
        a_1 = jax.random.normal(k4, (D, 1), dtype=jnp.float32)
        a_2 = jax.random.normal(k5, (D, 1), dtype=jnp.float32)
        a_3 = jax.random.normal(k6, (D, 1), dtype=jnp.float32)
        return {'hidden': hidden, 'adj': adj, 'a_0': a_0, 'a_1': a_1, 'a_2': a_2, 'a_3': a_3}
    _L3_gnn_all = _L3_gnn_setup()
    _L3_gnn_in = {k: v for k, v in _L3_gnn_all.items() if k in ('a_0', 'a_1', 'a_2', 'a_3')}
    del _L3_gnn_all
    return {'x': x, 'adj': adj, 'L0_gnn_W': _L0_gnn_in['W'], 'L0_gnn_b': _L0_gnn_in['b'], 'L1_gnn_W': _L1_gnn_in['W'], 'L1_gnn_a': _L1_gnn_in['a'], 'L2_gnn_W': _L2_gnn_in['W'], 'L2_gnn_a': _L2_gnn_in['a'], 'L2_gnn_bias': _L2_gnn_in['bias'], 'L3_gnn_a_0': _L3_gnn_in['a_0'], 'L3_gnn_a_1': _L3_gnn_in['a_1'], 'L3_gnn_a_2': _L3_gnn_in['a_2'], 'L3_gnn_a_3': _L3_gnn_in['a_3']}

def reference(x, adj, L0_gnn_W, L0_gnn_b, L1_gnn_W, L1_gnn_a, L2_gnn_W, L2_gnn_a, L2_gnn_bias, L3_gnn_a_0, L3_gnn_a_1, L3_gnn_a_2, L3_gnn_a_3):
    import jax
    import jax.numpy as jnp

    def _L0_gnn_ref(A, X, W, b):
        import jax, jax.numpy as jnp
        import numpy as np
        B, N, C, OUT, S = (4, 1024, 128, 128, 25)
        DENSITY = 0.008
        mask = A != 0
        neg_inf = jnp.float32(-jnp.inf)
        pri = -jnp.arange(N, dtype=jnp.float32)
        scores = jnp.where(mask, pri, neg_inf)
        vals, idx = jax.lax.top_k(scores, S)
        valid = vals > neg_inf
        feats = jax.vmap(lambda x, i: x[i])(X, idx)
        feats = jnp.where(valid[..., None], feats, neg_inf)
        agg = feats.max(axis=2)
        degree = mask.sum(axis=-1)
        agg = jnp.where((degree <= S)[..., None], jnp.maximum(agg, 0.0), agg)
        h = jnp.concatenate([X, agg], axis=-1)
        out = jax.nn.relu(jnp.einsum('bnf,fo->bno', h, W) + b)
        return out

    def _L1_gnn_ref(inp, adj, W, a):
        import jax, jax.numpy as jnp
        import numpy as np
        B, N, F_IN, F_OUT = (8, 1024, 128, 128)
        h = jnp.einsum('bnf,fo->bno', inp, W)
        a1 = a[:F_OUT, 0]
        a2 = a[F_OUT:, 0]
        s1 = h @ a1
        s2 = h @ a2
        e = jax.nn.leaky_relu(s1[:, :, None] + s2[:, None, :], negative_slope=0.4)
        att = jnp.where(adj > 0, e, jnp.float32(-1e+20))
        att = jax.nn.softmax(att, axis=1)
        h_prime = jnp.einsum('bij,bjo->bio', att, h)
        return jax.nn.gelu(h_prime, approximate=False)

    def _L2_gnn_ref(h, adj, W, a, bias):
        import jax, jax.numpy as jnp
        import numpy as np
        B, N, FIN, FOUT, H = (4, 512, 128, 128, 8)
        HID = FOUT // H
        ALPHA = 0.2
        NEG = -10000000000.0
        b, n = (h.shape[0], h.shape[1])
        hid = W.shape[1] // H
        s = (h @ W).reshape(b, n, H, hid)
        a_left, a_right = (a[:hid], a[hid:])
        e_i = jnp.einsum('bnhf,f->bnh', s, a_left)
        e_j = jnp.einsum('bnhf,f->bnh', s, a_right)
        e = e_i[:, :, None, :] + e_j[:, None, :, :]
        e = jnp.where(e > 0, e, ALPHA * e)
        masked = jnp.where(adj[..., None] == 0, NEG, e)
        att = jax.nn.softmax(masked, axis=1)
        h_prime = jnp.einsum('bijh,bjhf->bihf', att, s)
        out = h_prime.reshape(b, n, H * hid) + bias
        return out

    def _L3_gnn_ref(hidden, adj, a_0, a_1, a_2, a_3):
        import jax, jax.numpy as jnp
        import numpy as np
        LEAKY_SLOPE = 0.2
        NEG_INF = -9000000000000000.0

        def _edge_scores(h, a_k):
            e = jnp.einsum('bid,bjd->bij', h * a_k[:, 0], h)
            return jax.nn.leaky_relu(e, negative_slope=LEAKY_SLOPE)
        h = hidden
        e_0 = _edge_scores(h, a_0)
        e_1 = _edge_scores(h, a_1)
        e_2 = _edge_scores(h, a_2)
        e_3 = _edge_scores(h, a_3)
        scores = jnp.where(adj == 1, e_0, NEG_INF)
        scores = jnp.where(adj == 2, e_1, scores)
        scores = jnp.where(adj == 3, e_2, scores)
        scores = jnp.where(adj == 4, e_3, scores)
        alpha = jax.nn.softmax(scores, axis=-1)
        return jnp.einsum('bij,bjd->bid', alpha, h)
    h = jnp.maximum(_layernorm(x, axis=-1), 0.0)
    x = x + _L0_gnn_ref(adj, h, L0_gnn_W, L0_gnn_b)
    h = jnp.maximum(_layernorm(x, axis=-1), 0.0)
    x = x + _L1_gnn_ref(h, adj, L1_gnn_W, L1_gnn_a)
    h = jnp.maximum(_layernorm(x, axis=-1), 0.0)
    x = x + _L2_gnn_ref(h, adj, L2_gnn_W, L2_gnn_a, L2_gnn_bias)
    h = jnp.maximum(_layernorm(x, axis=-1), 0.0)
    x = x + _L3_gnn_ref(h, adj, L3_gnn_a_0, L3_gnn_a_1, L3_gnn_a_2, L3_gnn_a_3)
    return x

_drawn_inputs = setup_inputs


def setup_inputs(seed=0):
    import zlib

    import numpy as np

    out = dict(_drawn_inputs(seed))
    spreads = {'L0_gnn_b': (0.0, 0.1)}
    factors = {'L2_gnn_a': 8.0}
    for name, (base, spread) in spreads.items():
        noise = np.random.default_rng([zlib.crc32(name.encode()), seed]).standard_normal(out[name].shape)
        drawn = base * np.exp(spread * noise) if base else spread * noise
        out[name] = jnp.asarray(drawn.astype(out[name].dtype))
    for name, factor in factors.items():
        out[name] = (out[name] * factor).astype(out[name].dtype)
    return out
```

```python
from contextlib import ExitStack

import concourse.bass as bass
from concourse import mybir

ALU = mybir.AluOpType
ACT = mybir.ActivationFunctionType
AX = mybir.AxisListType
F32 = mybir.dt.float32
BF16 = mybir.dt.bfloat16
I32 = mybir.dt.int32
U16 = mybir.dt.uint16

P = 128
EPS = 1e-5
FIRST = 25
HEADS = 8
KINDS = 4
NEG = -float(2 ** 66)
LOWEST = -3.0e38
SLOPE1, SLOPE2, SLOPE3 = 0.4, 0.2, 0.2
PAD = 16


def graph_layers(nc, x, adj, W0, b0, W1, a1, W2, a2, bias2, a3, out):
    B, N, D = x.shape
    T = N // P
    HALF = N // 2
    HID = D // HEADS
    STRIDE = N + PAD
    ROUNDS = -(-FIRST // 8)

    A_USES = 5 + 2 * T
    A_H0, A_H1, A_H2, A_S2, A_H3, A_L3 = 0, 1, 2, 3, 4, 5
    B_USES = T // 2 + 2 + HEADS // 2 + 2 * T
    B_ADJ, B_AGG, B_U1, B_U2, B_L3 = 0, T // 2, T // 2 + 1, T // 2 + 2, T // 2 + 2 + HEADS // 2
    C_USES = T // 2 + 1 + HEADS // 2 + T
    C_ADJ, C_S1, C_U2, C_L3 = 0, T // 2, T // 2 + 1, T // 2 + 1 + HEADS // 2
    O_USES = 5 + T
    O_L0, O_V1, O_L1, O_V2, O_L2, O_L3 = range(6)
    W_USES = 8 + HEADS * T
    G_USES = 1 + T

    hrows = nc.dram_tensor("hrows", [B * STRIDE, D], F32, kind="Internal").ap()
    x_view = x.rearrange("b (t p) f -> b p t f", p=P)
    out_view = out.rearrange("b (t p) f -> b p t f", p=P)

    def flat(ap):
        return ap.rearrange("p a f -> p (a f)")

    with ExitStack() as ctx:
        def sb(name, shape, dt):
            return ctx.enter_context(nc.sbuf_tensor(name, shape, dt))

        def psum(name, shape, dt):
            return ctx.enter_context(nc.psum_tensor(name, shape, dt))

        def sem(name):
            return ctx.enter_context(nc.semaphore(name))

        identity = sb("identity", [P, P], F32)
        identity16 = sb("identity16", [P, P], BF16)
        ones = sb("ones", [P, P], F32)
        zeros = sb("zeros", [P, D], F32)
        countdown = sb("countdown", [P, N], F32)
        row_base = sb("row_base", [P, B], F32)
        w0_own = sb("w0_own", [D, D], F32)
        w0_agg = sb("w0_agg", [D, D], F32)
        b0_row = sb("b0_row", [1, D], F32)
        w1 = sb("w1", [D, D], F32)
        a1_all = sb("a1_all", [P, 2 * D], F32)
        w2 = sb("w2", [D, D], F32)
        a2_all = sb("a2_all", [P, 2 * HID], F32)
        bias2_row = sb("bias2_row", [1, HALF // D, D], F32)
        a3_cols = sb("a3_cols", [D, KINDS], F32)
        w1_left = sb("w1_left", [D, 1], F32)
        w1_right = sb("w1_right", [D, 1], F32)
        w2_left = sb("w2_left", [D, HEADS], F32)
        w2_right = sb("w2_right", [D, HEADS], F32)
        w1_left_rep = sb("w1_left_rep", [D, P], F32)
        w2_left_rep = sb("w2_left_rep", [D, HEADS, P], F32)

        xg = sb("xg", [P, T, D], F32)
        h = sb("h", [P, T, D], F32)
        hT = sb("hT", [D, N], F32)
        s = sb("s", [P, T, D], F32)
        adj_nat = sb("adj_nat", [P, T, N], BF16)
        adj_turned = sb("adj_turned", [P, T, N], BF16)
        agg = sb("agg", [P, T, D], F32)
        U = sb("U", [P, HEADS, N], F32)
        SU = sb("SU", [P, HEADS, N], F32)
        W = sb("W", [P, 8, N], F32)
        V = sb("V", [P, T, HEADS], F32)

        stats = sb("stats", [P, T, 6], F32)
        mean_var = sb("mean_var", [P, T, 2], F32)
        var_eps = sb("var_eps", [P, T], F32)
        std = sb("std", [P, T], F32)
        rstd = sb("rstd", [P, T], F32)
        minus_mean = sb("minus_mean", [P, T], F32)
        adj_prep = sb("adj_prep", [P, 2, N], I32)
        key = sb("key", [P, N], F32)
        top = sb("top", [P, 8 * ROUNDS], F32)
        index = sb("index", [P, 2, FIRST], I32)
        near = sb("near", [P, 2, FIRST, D], F32)
        mask_row = sb("mask_row", [P, 2, N], BF16)
        peak = sb("peak", [P, 8], F32)
        minus_max = sb("minus_max", [P, 8], F32)
        total = sb("total", [P, 8], F32)
        inv_total = sb("inv_total", [P, 8], F32)
        s_now = sb("s_now", [P, D], F32)
        peak3 = sb("peak3", [P, 2], F32)
        minus_max3 = sb("minus_max3", [P, 2], F32)
        total3 = sb("total3", [P, 2], F32)
        inv_total3 = sb("inv_total3", [P, 2], F32)
        adj_in = SU[:, 6:8, :].bitcast(I32)
        scaledT = U[:, 0, :].rearrange("p (q k i) -> p q k i", q=2, k=KINDS)
        kind_mask = U[:, 1:3, :].rearrange("p a n -> p (a n)").bitcast(U16).rearrange("p (k n) -> p k n", k=KINDS)
        aggT = W[:, 7, :]
        gelu_out = W[:, 0, :]
        probsT = [W[:, 4 + q, :].rearrange("p (t i) -> p t i", t=T) for q in range(2)]

        psA = psum("psA", [P, N], F32)
        psB = psum("psB", [P, N], F32)
        psC = psum("psC", [P, N], F32)
        acc = psum("acc", [P, N], F32)

        consts_loaded = sem("consts_loaded")
        all_x_loaded = sem("all_x_loaded")
        rows_stored = sem("rows_stored")
        graph_loaded = sem("graph_loaded")
        adj_in_loaded = [sem(f"adj_in_loaded{q}") for q in range(2)]
        adj_prep_loaded = [sem(f"adj_prep_loaded{q}") for q in range(2)]
        out_stored = sem("out_stored")
        gathered = [sem(f"gathered{q}") for q in range(2)]
        zeroed = sem("zeroed")
        consts_made = sem("consts_made")
        weights_made = sem("weights_made")
        first_var = sem("first_var")
        first_std = sem("first_std")
        first_scale = sem("first_scale")
        first_h = sem("first_h")
        var_ready = sem("var_ready")
        std_ready = sem("std_ready")
        scale_ready = sem("scale_ready")
        h_ready = sem("h_ready")
        hT_ready = sem("hT_ready")
        adj_in_used = sem("adj_in_used")
        adj_nat_ready = sem("adj_nat_ready")
        adj_turned_ready = sem("adj_turned_ready")
        adj_prep_used = sem("adj_prep_used")
        index_ready = sem("index_ready")
        agg_ready = sem("agg_ready")
        aggT_ready = sem("aggT_ready")
        A_full, A_free = sem("A_full"), sem("A_free")
        B_full, B_free = sem("B_full"), sem("B_free")
        C_full, C_free = sem("C_full"), sem("C_free")
        O_full, O_free = sem("O_full"), sem("O_free")
        u_ready = sem("u_ready")
        su_ready = sem("su_ready")
        v_ready = sem("v_ready")
        s_ready = sem("s_ready")
        shift_ready = sem("shift_ready")
        row_probs = sem("row_probs")
        row_used = sem("row_used")
        s_scaled = sem("s_scaled")
        gelu_in_ready = sem("gelu_in_ready")
        gelu_ready = sem("gelu_ready")
        x_updated = sem("x_updated")
        left_scaled = sem("left_scaled")
        selected = sem("selected")
        probs3 = sem("probs3")
        probsT_ready = sem("probsT_ready")
        passed = sem("passed")

        block = ctx.enter_context(nc.Block())

        @block.sync
        def _(sp):
            a1_row = a1.rearrange("n c -> (c n)")
            loads = [
                (w0_own[:], W0[0:D, :]), (w0_agg[:], W0[D:2 * D, :]),
                (b0_row[:], b0.rearrange("(c n) -> c n", c=1)),
                (w1[:], W1), (a1_all[:], a1_row.partition_broadcast(P)),
                (w2[:], W2), (a2_all[:], a2.partition_broadcast(P)),
            ]
            loads += [(bias2_row[:, c, :], bias2.rearrange("(c n) -> c n", c=1)) for c in range(HALF // D)]
            loads += [(a3_cols[:, k:k + 1], a3[k]) for k in range(KINDS)]
            for b in range(B):
                sp.dma_start(W[:, b, :].rearrange("p (t f) -> p t f", t=T), x_view[b]).then_inc(all_x_loaded, 16)
            for dst, src in loads:
                sp.dma_start(dst, src).then_inc(consts_loaded, 16)

            def load_prep_tile(b, t):
                sp.wait_ge(adj_prep_used, b * T + (t + 1))
                sp.dma_start(adj_prep[:, t % 2, :], adj[b, t * P:(t + 1) * P, :]).then_inc(adj_prep_loaded[t % 2], 16)

            load_prep_tile(0, 0)
            load_prep_tile(0, 1)
            sp.wait_ge(first_h, B)
            for b in range(B):
                sp.dma_start(hrows[b * STRIDE:b * STRIDE + N, :].rearrange("(t p) f -> p t f", p=P),
                             U[:, b, :].rearrange("p (t f) -> p t f", t=T)).then_inc(rows_stored, 16)
            sp.wait_ge(zeroed, 3)
            for b in range(B):
                sp.dma_start(hrows[b * STRIDE + N:(b + 1) * STRIDE, :], zeros[0:PAD, :]).then_inc(rows_stored, 16)
            for t in range(2, T):
                load_prep_tile(0, t)
            sp.wait_ge(rows_stored, 2 * B * 16)

            def graph(b, prep):
                sp.dma_start(xg[:], x_view[b]).then_inc(graph_loaded, 16)
                sp.dma_start(h[:], hrows[bass.ds(b * STRIDE, N), :].rearrange("(t p) f -> p t f", p=P))\
                    .then_inc(graph_loaded, 16)
                for t in range(T):
                    sp.wait_ge(adj_in_used, b * T + (t + 1))
                    sp.dma_start(adj_in[:, t % 2, :], adj[b, t * P:(t + 1) * P, :]).then_inc(adj_in_loaded[t % 2], 16)
                if prep:
                    for t in range(T):
                        load_prep_tile(b + 1, t)
                sp.wait_ge(x_updated, b * 4 + 4)
                sp.dma_start(out_view[b], xg[:]).then_inc(out_stored, 16)
                sp.wait_ge(out_stored, b * 16 + 16)
                sp.sem_inc(passed, 1)

            with sp.Fori(0, B - 1) as b:
                graph(b, True)
            graph(B - 1, False)

        @block.gpsimd
        def _(pool):
            nc.gpsimd.memset(identity[:], 0.0).then_inc(zeroed, 1)
            nc.gpsimd.memset(identity16[:], 0.0).then_inc(zeroed, 1)
            nc.gpsimd.memset(zeros[:], 0.0).then_inc(zeroed, 1)
            nc.gpsimd.memset(ones[:], 1.0).then_inc(consts_made, 1)
            pool.wait_ge(zeroed, 3)
            for m in (identity, identity16):
                nc.gpsimd.affine_select(out=m[:], in_=m[:], compare_op=ALU.not_equal, fill=1.0, base=0,
                                        pattern=[[-1, P]], channel_multiplier=1).then_inc(consts_made, 1)
            nc.gpsimd.iota(countdown[:], pattern=[[-1, N]], base=N, channel_multiplier=0,
                           allow_small_or_imprecise_dtypes=True).then_inc(consts_made, 1)
            nc.gpsimd.iota(row_base[:], pattern=[[STRIDE, B]], base=N, channel_multiplier=0,
                           allow_small_or_imprecise_dtypes=True).then_inc(consts_made, 1)
            pool.wait_ge(rows_stored, 2 * B * 16)
            with pool.Fori(0, B * T // 2) as pair:
                for q in range(2):
                    pool.wait_ge(index_ready, pair * 2 + (q + 1))
                    pool.sem_inc(passed, 1)
                    for k in range(FIRST):
                        nc.gpsimd.indirect_dma_start(
                            out=near[:, q, k, :], out_offset=None, in_=hrows,
                            in_offset=bass.IndirectOffsetOnAxis(ap=index[:, q, k:k + 1], axis=0)
                        ).then_inc(gathered[q], 16)

        @block.vector
        def _(dve):
            dve.sem_inc(adj_prep_used, 2)

            def norm_stats(xv, ready, made, count, scaled):
                for t in range(T):
                    nc.vector.bn_stats(stats[:, t, :], xv[:, t, :])
                dve.drain()
                for t in range(T):
                    nc.vector.bn_aggr(mean_var[:, t, :], stats[:, t, :])
                dve.drain()
                nc.vector.tensor_scalar(var_eps[:], mean_var[:, :, 1], EPS, None, ALU.add).then_inc(ready, 1)
                dve.wait_ge(made, count)
                nc.vector.reciprocal(rstd[:], std[:])
                dve.drain()
                nc.vector.scalar_tensor_tensor(out=minus_mean[:], in0=mean_var[:, :, 0], scalar=-1.0,
                                               in1=rstd[:], op0=ALU.mult, op1=ALU.mult).then_inc(scaled, 1)

            for b in range(B):
                dve.wait_ge(all_x_loaded, B * 16)
                if b:
                    dve.wait_ge(first_h, b)
                norm_stats(W[:, b, :].rearrange("p (t f) -> p t f", t=T), first_var, first_std, b + 1, first_scale)

            dve.wait_ge(consts_loaded, (7 + HALF // D + KINDS) * 16)
            dve.wait_ge(consts_made, 5)
            for col, a_part in ((w1_left, a1_all[:, 0:D]), (w1_right, a1_all[:, D:2 * D])):
                nc.vector.tensor_tensor(key[:, 0:D], w1[:], a_part, ALU.mult)
                dve.drain()
                nc.vector.reduce_sum(col[:], key[:, 0:D], AX.X)
                dve.drain()
            for cols, a_part in ((w2_left, a2_all[:, 0:HID]), (w2_right, a2_all[:, HID:2 * HID])):
                prod = key[:, 0:D].rearrange("p (h e) -> p h e", h=HEADS)
                for hd in range(HEADS):
                    nc.vector.tensor_tensor(prod[:, hd, :], w2[:, hd * HID:(hd + 1) * HID], a_part, ALU.mult)
                dve.drain()
                nc.vector.reduce_sum(cols[:], prod, AX.X)
                dve.drain()
            nc.vector.tensor_scalar(w1_left_rep[:], ones[:], w1_left[:, 0:1], None, ALU.mult)
            for hd in range(HEADS):
                nc.vector.tensor_scalar(w2_left_rep[:, hd, :], ones[:], w2_left[:, hd:hd + 1], None, ALU.mult)
            dve.drain()
            nc.vector.memset(peak[:], 0.0).then_inc(weights_made, 1)

            def neighbour_list(b, t, q):
                dve.wait_ge(adj_prep_loaded[q], b * (16 * T // 2) + (t - q) * 8 + 16)
                dve.sem_inc(passed, 1)
                nc.vector.scalar_tensor_tensor(out=key[:], in0=adj_prep[:, q, :], scalar=0.0, in1=countdown[:],
                                               op0=ALU.not_equal, op1=ALU.mult).then_inc(adj_prep_used, 1)
                dve.drain()
                for r in range(ROUNDS):
                    nc.vector.max(out=top[:, 8 * r:8 * r + 8], in_=key[:])
                    dve.drain()
                    if r < ROUNDS - 1:
                        nc.vector.match_replace(out=key[:], in_to_replace=top[:, 8 * r:8 * r + 8],
                                                in_values=key[:], imm_value=0.0)
                        dve.drain()
                nc.vector.tensor_scalar(index[:, q, :], top[:, 0:FIRST], -1.0, row_base[:, bass.ds(b, 1)],
                                        ALU.mult, ALU.add).then_inc(index_ready, 1)

            def neighbour_max(b, t, q):
                dve.wait_ge(gathered[q], (b * (T // 2) * FIRST + FIRST) * 16 + (t - q) * (FIRST * 8))
                nc.vector.reduce_max(agg[:, bass.ds(t, 1), :].rearrange("p a f -> p (a f)"),
                                     near[:, q, :, :].rearrange("p k f -> p f k"), AX.X).then_inc(agg_ready, 1)

            neighbour_list(0, 0, 0)
            for t in range(1, T):
                neighbour_list(0, t, t % 2)
                neighbour_max(0, t - 1, (t - 1) % 2)

            def normalise(b, layer):
                norm_stats(xg[:], var_ready, std_ready, b * 3 + layer, scale_ready)

            def leaky_scores(slot, hd, v_col):
                nc.vector.scalar_tensor_tensor(out=W[:, slot, :], in0=U[:, hd, :], scalar=v_col, in1=SU[:, hd, :],
                                               op0=ALU.add, op1=ALU.max)

            def mask_scores(slot, mask):
                nc.vector.tensor_tensor_reduce(out=W[:, slot, :], in0=W[:, slot, :], in1=mask, scale=1.0,
                                               scalar=LOWEST, op0=ALU.add, op1=ALU.max,
                                               accum_out=peak[:, slot:slot + 1])

            def shifts():
                nc.vector.tensor_scalar(minus_max[:], peak[:], -1.0, None, ALU.mult).then_inc(shift_ready, 1)

            def update_x(src, b, layer):
                nc.vector.tensor_tensor(flat(xg[:]), src, flat(xg[:]), ALU.add).then_inc(x_updated, 1)

            def graph(b, prep):
                neighbour_max(b, T - 1, 1)
                dve.wait_ge(graph_loaded, b * 32 + 32)
                dve.wait_ge(O_full, b * O_USES + O_L0 + 1)
                nc.vector.scalar_tensor_tensor(out=flat(xg[:]), in0=acc[:], scalar=0.0, in1=flat(xg[:]),
                                               op0=ALU.max, op1=ALU.add).then_inc(x_updated, 1)
                dve.wait_ge(x_updated, b * 4 + 1)
                dve.sem_inc(O_free, 1)

                normalise(b, 1)
                dve.wait_ge(adj_turned_ready, b * T + T)
                dve.wait_ge(u_ready, b * (1 + HEADS) + 1)
                dve.wait_ge(v_ready, b * 2 + 1)
                for jt in range(T):
                    leaky_scores(jt, 0, V[:, jt, 0:1])
                for jt in range(T):
                    nc.vector.tensor_scalar(mask_row[:, jt % 2, :], adj_turned[:, jt, :], 0.0, NEG,
                                            ALU.is_le, ALU.mult)
                    dve.drain()
                    mask_scores(jt, mask_row[:, jt % 2, :])
                dve.drain()
                shifts()
                dve.wait_ge(s_ready, b * 2 + 1)
                dve.wait_ge(row_probs, b * W_USES + 8)
                nc.vector.reciprocal(inv_total[:], total[:])
                dve.drain()
                for jt in range(T):
                    last = nc.vector.tensor_scalar(s[:, jt, :], s[:, jt, :], inv_total[:, jt:jt + 1], None, ALU.mult)
                last.then_inc(s_scaled, 1)
                dve.wait_ge(gelu_ready, b + 1)
                update_x(gelu_out, b, 1)
                dve.wait_ge(x_updated, b * 4 + 2)

                normalise(b, 2)
                dve.wait_ge(v_ready, b * 2 + 2)
                dve.wait_ge(s_ready, b * 2 + 2)
                dve.wait_ge(u_ready, b * (1 + HEADS) + 1 + HEADS)

                def finish_tile(jt):
                    dve.wait_ge(row_probs, b * W_USES + jt * HEADS + 8 + HEADS)
                    nc.vector.reciprocal(inv_total[:], total[:])
                    dve.drain()
                    dve.wait_ge(row_used, b * W_USES + jt * HEADS + 8)
                    for hd in range(HEADS):
                        last = nc.vector.tensor_scalar(s_now[:, hd * HID:(hd + 1) * HID],
                                                       s[:, bass.ds(jt, 1), hd * HID:(hd + 1) * HID].rearrange("p a e -> p (a e)"),
                                                       inv_total[:, hd:hd + 1], None, ALU.mult)
                    last.then_inc(s_scaled, 1)

                def mask_tile(jt):
                    nc.vector.tensor_scalar(mask_row[:, 0, :], adj_turned[:, bass.ds(jt, 1), :].rearrange("p a n -> p (a n)"),
                                            0.0, NEG, ALU.is_equal, ALU.mult)
                    for hd in range(HEADS):
                        dve.wait_ge(row_used, b * W_USES + jt * HEADS + (hd + 1))
                        leaky_scores(hd, hd, V[:, bass.ds(jt, 1), hd:hd + 1].rearrange("p a e -> p (a e)"))
                    dve.drain()
                    for hd in range(HEADS):
                        mask_scores(hd, mask_row[:, 0, :])
                    dve.drain()
                    dve.wait_ge(row_probs, b * W_USES + jt * HEADS + 8)
                    shifts()

                if prep:
                    neighbour_list(b + 1, 0, 0)
                    with dve.Fori(0, T // 2 - 1) as pair:
                        for q in range(2):
                            jt = pair * 2 + q
                            mask_tile(jt)
                            neighbour_list(b + 1, jt + 1, 1 - q)
                            finish_tile(jt)
                            neighbour_max(b + 1, jt, q)
                    mask_tile(T - 2)
                    neighbour_list(b + 1, T - 1, 1)
                    finish_tile(T - 2)
                    neighbour_max(b + 1, T - 2, 0)
                    mask_tile(T - 1)
                    finish_tile(T - 1)
                else:
                    with dve.Fori(0, T) as jt:
                        mask_tile(jt)
                        finish_tile(jt)
                dve.wait_ge(O_full, b * O_USES + O_L2 + 1)
                update_x(acc[:], b, 2)
                dve.wait_ge(x_updated, b * 4 + 3)
                dve.sem_inc(O_free, 1)

                normalise(b, 3)
                dve.wait_ge(hT_ready, b * 4 + 4)

                def scale_left(it, q):
                    dve.wait_ge(B_full, b * B_USES + it * 2 + (B_L3 - 2))
                    for k in range(KINDS):
                        last = nc.vector.tensor_scalar(scaledT[:, q, k, :], hT[:, bass.ds(it * P, P)],
                                                       a3_cols[:, k:k + 1], None, ALU.mult)
                    last.then_inc(left_scaled, 1)

                def select(it, q):
                    nat = adj_nat[:, bass.ds(it, 1), :].rearrange("p a n -> p (a n)")
                    dve.wait_ge(C_full, b * C_USES + it + (C_L3 - 1))
                    nc.vector.tensor_scalar(mask_row[:, 1, :], nat, 1.0, NEG, ALU.not_equal, ALU.mult)
                    for k in range(1, KINDS):
                        nc.vector.tensor_scalar(kind_mask[:, k, :], nat, k + 1.0, None, ALU.is_equal)
                    dve.drain()
                    for k in range(KINDS):
                        full, free, ps = ((A_full, A_free, psA), (B_full, B_free, psB))[k % 2]
                        base = b * (A_USES, B_USES)[k % 2] + it * 2 + ((A_L3, B_L3)[k % 2] + k // 2 + 1)
                        dve.wait_ge(full, base)
                        if k == 0:
                            nc.vector.tensor_tensor(W[:, q, :], ps[:], mask_row[:, 1, :], ALU.add).then_inc(free, 1)
                        else:
                            dve.sem_inc(passed, 1)
                            nc.vector.copy_predicated(W[:, q, :], kind_mask[:, k, :], ps[:]).then_inc(free, 1)
                        dve.drain()
                    nc.vector.scalar_tensor_tensor(out=W[:, q, :], in0=W[:, q, :], scalar=SLOPE3, in1=W[:, q, :],
                                                   op0=ALU.mult, op1=ALU.max)
                    dve.drain()
                    nc.vector.reduce_max(peak3[:, q:q + 1], W[:, q, :], AX.X)
                    dve.drain()
                    nc.vector.tensor_scalar(minus_max3[:, q:q + 1], peak3[:, q:q + 1], -1.0, None,
                                            ALU.mult).then_inc(selected, 1)

                def finish_rows(it, q):
                    dve.wait_ge(probs3, b * T + it + 1)
                    nc.vector.reciprocal(inv_total3[:, q:q + 1], total3[:, q:q + 1])
                    dve.drain()
                    dve.wait_ge(O_full, b * O_USES + it + (O_L3 + 1))
                    xt = xg[:, bass.ds(it, 1), :].rearrange("p a f -> p (a f)")
                    nc.vector.scalar_tensor_tensor(out=xt, in0=acc[:, q * HALF:q * HALF + D], scalar=inv_total3[:, q:q + 1],
                                                   in1=xt, op0=ALU.mult, op1=ALU.add).then_inc(O_free, 1)

                scale_left(0, 0)
                scale_left(1, 1)
                select(0, 0)
                with dve.Fori(0, T // 2 - 1) as pair:
                    it = pair * 2
                    scale_left(it + 2, 0)
                    select(it + 1, 1)
                    finish_rows(it, 0)
                    scale_left(it + 3, 1)
                    select(it + 2, 0)
                    finish_rows(it + 1, 1)
                select(T - 1, 1)
                finish_rows(T - 2, 0)
                finish_rows(T - 1, 1)
                dve.drain()
                nc.vector.memset(peak[:, 0:1], 0.0).then_inc(x_updated, 1)

            with dve.Fori(0, B - 1) as b:
                graph(b, True)
            graph(B - 1, False)

        @block.scalar
        def _(act):
            act.sem_inc(adj_in_used, 2)
            for b in range(B):
                act.wait_ge(first_var, b + 1)
                nc.scalar.activation(std[:], var_eps[:], ACT.Sqrt).then_inc(first_std, 1)
                act.wait_ge(first_scale, b + 1)
                for t in range(T):
                    last = nc.scalar.activation(U[:, b, t * D:(t + 1) * D], W[:, b, t * D:(t + 1) * D], ACT.Relu,
                                                bias=minus_mean[:, t:t + 1], scale=rstd[:, t:t + 1])
                last.then_inc(first_h, 1)

            def copy_out(dst, src, full, count, free, ready):
                act.wait_ge(full, count)
                nc.scalar.copy(dst, src).then_inc(ready, 1)
                return free

            def graph(b):
                for t in range(T):
                    act.wait_ge(adj_in_loaded[t % 2], b * (16 * T // 2) + (t // 2 + 1) * 16)
                    nc.scalar.copy(adj_nat[:, t, :], adj_in[:, t % 2, :]).then_inc(adj_nat_ready, 1)
                    act.wait_ge(adj_nat_ready, b * T + (t + 1))
                    act.sem_inc(adj_in_used, 1)

                def turn(full, count, src, dst, free, ready, ready_count):
                    act.wait_ge(full, count)
                    nc.scalar.copy(dst, src).then_inc(ready, 1)
                    act.wait_ge(ready, ready_count)
                    act.sem_inc(free, 1)

                turn(A_full, b * A_USES + A_H0 + 1, psA[:], hT[:], A_free, hT_ready, b * 4 + 1)
                for jt in range(T):
                    ps, full, free, uses = ((psB, B_full, B_free, B_USES), (psC, C_full, C_free, C_USES))[jt % 2]
                    turn(full, b * uses + jt // 2 + 1, ps[:, 0:HALF].bitcast(BF16), adj_turned[:, jt, :], free,
                         adj_turned_ready, b * T + jt + 1)
                turn(B_full, b * B_USES + B_AGG + 1, psB[:], aggT, B_free, aggT_ready, b + 1)

                def normalise(layer, a_use):
                    act.wait_ge(var_ready, b * 3 + layer)
                    nc.scalar.activation(std[:], var_eps[:], ACT.Sqrt).then_inc(std_ready, 1)
                    act.wait_ge(scale_ready, b * 3 + layer)
                    for t in range(T):
                        last = nc.scalar.activation(h[:, t, :], xg[:, t, :], ACT.Relu, bias=minus_mean[:, t:t + 1],
                                                    scale=rstd[:, t:t + 1])
                    last.then_inc(h_ready, 1)
                    turn(A_full, b * A_USES + a_use + 1, psA[:], hT[:], A_free, hT_ready, b * 4 + layer + 1)

                def probabilities(group):
                    act.wait_ge(shift_ready, b * G_USES + group)
                    for q in range(8):
                        nc.scalar.activation(W[:, q, :], W[:, q, :], ACT.Exp, bias=minus_max[:, q:q + 1],
                                             accum_out=total[:, q:q + 1]).then_inc(row_probs, 1)

                def turn_scores(full, count, ps, hd, free, slope, n):
                    act.wait_ge(full, count)
                    nc.scalar.mul(SU[:, hd, :], ps[:], slope).then_inc(su_ready, 1)
                    act.wait_ge(su_ready, b * (1 + HEADS) + n)
                    turn(full, count, ps[:], U[:, hd, :], free, u_ready, b * (1 + HEADS) + n)

                def turn_right(count, src, dst, slope):
                    act.wait_ge(O_full, count)
                    nc.scalar.mul(dst, src, 1.0 - slope).then_inc(v_ready, 1)

                normalise(1, A_H1)
                turn_scores(B_full, b * B_USES + B_U1 + 1, psB, 0, B_free, SLOPE1, 1)
                turn(C_full, b * C_USES + C_S1 + 1, psC[:], flat(s[:]), C_free, s_ready, b * 2 + 1)
                turn_right(b * O_USES + O_V1 + 1, acc[:, 0:T], V[:, :, 0], SLOPE1)
                act.wait_ge(v_ready, b * 2 + 1)
                act.sem_inc(O_free, 1)
                probabilities(1)
                turn(O_full, b * O_USES + O_L1 + 1, acc[:], W[:, 1, :], O_free, gelu_in_ready, b + 1)
                nc.scalar.activation(gelu_out, W[:, 1, :], ACT.Gelu).then_inc(gelu_ready, 1)

                normalise(2, A_H2)
                for hd in range(HEADS):
                    ps, full, free, count = ((psB, B_full, B_free, b * B_USES + B_U2 + (hd // 2 + 1)),
                                             (psC, C_full, C_free, b * C_USES + C_U2 + (hd // 2 + 1)))[hd % 2]
                    turn_scores(full, count, ps, hd, free, SLOPE2, hd + 2)
                turn(A_full, b * A_USES + A_S2 + 1, psA[:], flat(s[:]), A_free, s_ready, b * 2 + 2)
                turn_right(b * O_USES + O_V2 + 1, acc[:, 0:T * HEADS], V[:].rearrange("p t h -> p (t h)"), SLOPE2)
                act.wait_ge(v_ready, b * 2 + 2)
                act.sem_inc(O_free, 1)
                with act.Fori(0, T) as jt:
                    probabilities(jt + 2)

                normalise(3, A_H3)
                with act.Fori(0, T // 2) as pair:
                    for q in range(2):
                        it = pair * 2 + q
                        act.wait_ge(selected, b * T + it + 1)
                        nc.scalar.activation(W[:, q, :], W[:, q, :], ACT.Exp, bias=minus_max3[:, q:q + 1],
                                             accum_out=total3[:, q:q + 1]).then_inc(probs3, 1)
                        act.wait_ge(O_full, b * O_USES + it + (O_L3 - 1))
                        turn(C_full, b * C_USES + it + (C_L3 + 1), psC[:], flat(probsT[q]), C_free, probsT_ready,
                             b * T + it + 1)
                act.wait_ge(x_updated, b * 4 + 4)

            with act.Fori(0, B) as b:
                graph(b)

        @block.tensor
        def _(pe):
            for free in (A_free, B_free, C_free, O_free):
                pe.sem_inc(free, 1)
            pe.wait_ge(consts_made, 5)
            pe.wait_ge(weights_made, 1)
            pe.wait_ge(consts_loaded, (7 + HALF // D + KINDS) * 16)

            def mm(dst, lhsT, rhs, start=True, stop=True):
                return nc.tensor.matmul(dst, lhsT, rhs, start=start, stop=stop, skip_group_check=True)

            def turn_tiles(dst, src, full):
                for t in range(T):
                    last = nc.tensor.transpose(dst[:, t * P:(t + 1) * P], src(t), identity[:])
                last.then_inc(full, 1)

            def graph(b):
                pe.wait_ge(graph_loaded, b * 32 + 32)
                pe.wait_ge(A_free, b * A_USES + A_H0 + 1)
                turn_tiles(psA, lambda t: h[:, t, :], A_full)
                pe.wait_ge(adj_nat_ready, b * T + T)
                for jt in range(T):
                    ps, full, free, uses = ((psB, B_full, B_free, B_USES), (psC, C_full, C_free, C_USES))[jt % 2]
                    pe.wait_ge(free, b * uses + (jt // 2 + 1))
                    dst = ps[:, 0:HALF].bitcast(BF16)
                    for it in range(T):
                        last = nc.tensor.transpose(dst[:, it * P:(it + 1) * P], adj_nat[:, it, jt * P:(jt + 1) * P],
                                                   identity16[:])
                    last.then_inc(full, 1)
                pe.wait_ge(agg_ready, b * T + T)
                pe.wait_ge(B_free, b * B_USES + B_AGG + 1)
                turn_tiles(psB, lambda t: agg[:, t, :], B_full)
                pe.wait_ge(hT_ready, b * 4 + 1)
                pe.wait_ge(aggT_ready, b + 1)
                pe.wait_ge(O_free, b * O_USES + O_L0 + 1)
                for t in range(T):
                    dst = acc[:, t * D:(t + 1) * D]
                    mm(dst, hT[:, t * P:(t + 1) * P], w0_own[:], True, False)
                    mm(dst, aggT[:, t * P:(t + 1) * P], w0_agg[:], False, False)
                    last = mm(dst, ones[0:1, :], b0_row[:], False, True)
                last.then_inc(O_full, 1)

                def turn_h(layer, a_use):
                    pe.wait_ge(h_ready, b * 3 + layer)
                    pe.wait_ge(A_free, b * A_USES + a_use + 1)
                    turn_tiles(psA, lambda t: h[:, t, :], A_full)
                    pe.wait_ge(hT_ready, b * 4 + layer + 1)

                def spread(ps, rep, full):
                    for c in range(2):
                        last = mm(ps[:, c * HALF:(c + 1) * HALF], rep, hT[:, c * HALF:(c + 1) * HALF])
                    last.then_inc(full, 1)

                def project(ps, weight, full):
                    n = weight.shape[1]
                    for t in range(T):
                        last = mm(ps[:, t * n:(t + 1) * n], hT[:, t * P:(t + 1) * P], weight)
                    last.then_inc(full, 1)

                turn_h(1, A_H1)
                pe.wait_ge(B_free, b * B_USES + B_U1 + 1)
                spread(psB, w1_left_rep[:], B_full)
                pe.wait_ge(C_free, b * C_USES + C_S1 + 1)
                project(psC, w1[:], C_full)
                pe.wait_ge(O_free, b * O_USES + O_V1 + 1)
                project(acc, w1_right[:], O_full)
                pe.wait_ge(s_scaled, b * G_USES + 1)
                pe.wait_ge(row_probs, b * W_USES + 8)
                pe.wait_ge(O_free, b * O_USES + O_L1 + 1)
                for it in range(T):
                    for jt in range(T):
                        last = mm(acc[:, it * D:(it + 1) * D], W[:, jt, it * P:(it + 1) * P], s[:, jt, :],
                                  jt == 0, jt == T - 1)
                last.then_inc(O_full, 1)

                turn_h(2, A_H2)
                for hd in range(HEADS):
                    ps, full, free, count = ((psB, B_full, B_free, b * B_USES + B_U2 + (hd // 2 + 1)),
                                             (psC, C_full, C_free, b * C_USES + C_U2 + (hd // 2 + 1)))[hd % 2]
                    pe.wait_ge(free, count)
                    spread(ps, w2_left_rep[:, hd, :], full)
                pe.wait_ge(A_free, b * A_USES + A_S2 + 1)
                project(psA, w2[:], A_full)
                pe.wait_ge(O_free, b * O_USES + O_V2 + 1)
                project(acc, w2_right[:], O_full)
                pe.wait_ge(gelu_ready, b + 1)
                pe.sem_inc(row_used, 8)
                pe.wait_ge(O_free, b * O_USES + O_L2 + 1)
                for c in range(2):
                    mm(acc[:, c * HALF:(c + 1) * HALF], ones[0:1, :], bias2_row[:].rearrange("p c n -> p (c n)"),
                       True, False)
                with pe.Fori(0, T) as jt:
                    pe.wait_ge(s_scaled, b * G_USES + jt + 2)
                    for hd in range(HEADS):
                        for it in range(T):
                            lo = it * D + hd * HID
                            last = mm(acc[:, lo:lo + HID], W[:, hd, it * P:(it + 1) * P],
                                      s_now[:, hd * HID:(hd + 1) * HID], False, False)
                        last.then_inc(row_used, 1)
                pe.wait_ge(row_used, b * W_USES + W_USES)
                pe.sem_inc(O_full, 1)

                turn_h(3, A_H3)

                def scores(it, q):
                    pe.wait_ge(left_scaled, b * T + it + 1)
                    for k in range(KINDS):
                        ps, full, free, uses, first = ((psA, A_full, A_free, A_USES, A_L3),
                                                       (psB, B_full, B_free, B_USES, B_L3))[k % 2]
                        pe.wait_ge(free, b * uses + it * 2 + (first + k // 2 + 1))
                        spread(ps, scaledT[:, q, k, :], full)

                def combine(it, q):
                    pe.wait_ge(probs3, b * T + it + 1)
                    pe.wait_ge(C_free, b * C_USES + it + (C_L3 + 1))
                    turn_tiles(psC, lambda t: W[:, q, t * P:(t + 1) * P], C_full)
                    pe.wait_ge(probsT_ready, b * T + it + 1)
                    pe.wait_ge(O_free, b * O_USES + it + O_L3)
                    for jt in range(T):
                        last = mm(acc[:, q * HALF:q * HALF + D], probsT[q][:, jt, :], h[:, jt, :], jt == 0, jt == T - 1)
                    last.then_inc(O_full, 1)

                scores(0, 0)
                with pe.Fori(0, T // 2 - 1) as pair:
                    it = pair * 2
                    scores(it + 1, 1)
                    combine(it, 0)
                    scores(it + 2, 0)
                    combine(it + 1, 1)
                scores(T - 1, 1)
                combine(T - 2, 0)
                combine(T - 1, 1)

            with pe.Fori(0, B) as b:
                graph(b)


_INS = ['x', 'adj', 'L0_gnn_W', 'L0_gnn_b', 'L1_gnn_W', 'L1_gnn_a', 'L2_gnn_W', 'L2_gnn_a', 'L2_gnn_bias',
        'L3_gnn_a_0', 'L3_gnn_a_1', 'L3_gnn_a_2', 'L3_gnn_a_3']


def kernel(**inputs):
    import numpy as _np
    import concourse.bacc as _bacc
    from concourse.bass_utils import run_bass_kernel_spmd as _run

    nc = _bacc.Bacc("TRN2", target_bir_lowering=False, num_devices=1)
    arrays, args = {}, []
    for name in _INS:
        a = _np.ascontiguousarray(inputs[name])
        arrays[f"in_{name}_dram"] = a
        args.append(nc.dram_tensor(f"in_{name}_dram", a.shape, mybir.dt.from_np(a.dtype), kind="ExternalInput").ap())
    out = nc.dram_tensor("out_0_dram", inputs['x'].shape, F32, kind="ExternalOutput").ap()
    graph_layers(nc, *args[:9], args[9:], out)
    r = _run(nc, [arrays], core_ids=[0])
    return r.results[0]["out_0_dram"]
```

```python
from contextlib import ExitStack

import concourse.bass as bass
from concourse import mybir

ALU = mybir.AluOpType
ACT = mybir.ActivationFunctionType
AX = mybir.AxisListType
F32 = mybir.dt.float32
BF16 = mybir.dt.bfloat16
I32 = mybir.dt.int32
U16 = mybir.dt.uint16

P = 128
EPS = 1e-5
FIRST = 25
HEADS = 8
KINDS = 4
NEG = -float(2 ** 66)
LOWEST = -3.0e38
SLOPE1, SLOPE2, SLOPE3 = 0.4, 0.2, 0.2
PAD = 16


def graph_layers(nc, x, adj, W0, b0, W1, a1, W2, a2, bias2, a3, out):
    B, N, D = x.shape
    T = N // P
    HALF = N // 2
    HID = D // HEADS
    STRIDE = N + PAD
    ROUNDS = -(-FIRST // 8)
    PARTS = (range(0, (FIRST + 1) // 2), range((FIRST + 1) // 2, FIRST))

    A_USES = 5 + 2 * T
    A_H0, A_H1, A_H2, A_S2, A_H3, A_L3 = 0, 1, 2, 3, 4, 5
    B_USES = T // 2 + 2 + HEADS // 2 + 2 * T
    B_AGG, B_ADJ, B_U1, B_U2, B_L3 = 0, 1, T // 2 + 1, T // 2 + 2, T // 2 + 2 + HEADS // 2
    C_USES = T // 2 + 1 + HEADS // 2 + T
    C_ADJ, C_S1, C_U2, C_L3 = 0, T // 2, T // 2 + 1, T // 2 + 1 + HEADS // 2
    O_USES = 5 + T
    O_L0, O_V1, O_L1, O_V2, O_L2, O_L3 = range(6)
    W_USES = 8 + HEADS * T
    G_USES = 2 + 2 * T

    hrows = nc.dram_tensor("hrows", [B * STRIDE, D], F32, kind="Internal").ap()
    x_view = x.rearrange("b (t p) f -> b p t f", p=P)
    out_view = out.rearrange("b (t p) f -> b p t f", p=P)

    def flat(ap):
        return ap.rearrange("p a f -> p (a f)")

    with ExitStack() as ctx:
        def sb(name, shape, dt):
            return ctx.enter_context(nc.sbuf_tensor(name, shape, dt))

        def psum(name, shape, dt):
            return ctx.enter_context(nc.psum_tensor(name, shape, dt))

        def sem(name):
            return ctx.enter_context(nc.semaphore(name))

        identity = sb("identity", [P, P], F32)
        identity16 = sb("identity16", [P, P], BF16)
        ones = sb("ones", [P, P], F32)
        zeros = sb("zeros", [PAD, D], F32)
        countdown = sb("countdown", [P, N], U16)
        row_base = sb("row_base", [P, B], F32)
        w0_own = sb("w0_own", [D, D], F32)
        w0_agg = sb("w0_agg", [D, D], F32)
        b0_row = sb("b0_row", [1, D], F32)
        w1 = sb("w1", [D, D], F32)
        a1_all = sb("a1_all", [P, 2 * D], F32)
        w2 = sb("w2", [D, D], F32)
        a2_all = sb("a2_all", [P, 2 * HID], F32)
        bias2_row = sb("bias2_row", [1, D], F32)
        a3_cols = sb("a3_cols", [D, KINDS], F32)
        w1_left = sb("w1_left", [D, 1], F32)
        w1_right = sb("w1_right", [D, 1], F32)
        w2_left = sb("w2_left", [D, HEADS], F32)
        w2_right = sb("w2_right", [D, HEADS], F32)
        w1_left_rep = sb("w1_left_rep", [D, P], F32)
        w2_left_rep = sb("w2_left_rep", [D, HEADS, P], F32)

        xg = sb("xg", [P, T, D], F32)
        h = sb("h", [P, T, D], F32)
        hT = sb("hT", [D, N], F32)
        s = sb("s", [P, T, D], F32)
        adj_nat = sb("adj_nat", [P, 2, T, N], BF16)
        adj_turned = sb("adj_turned", [P, T, N], BF16)
        agg = sb("agg", [P, T, D], F32)
        U = sb("U", [P, HEADS, N], F32)
        SU = sb("SU", [P, HEADS, N], F32)
        W = sb("W", [P, 8, N], F32)
        V = sb("V", [P, T, HEADS], F32)

        stats = sb("stats", [P, T, 6], F32)
        mean_var = sb("mean_var", [P, T, 2], F32)
        var_eps = sb("var_eps", [P, T], F32)
        std = sb("std", [P, T], F32)
        rstd = sb("rstd", [P, T], F32)
        minus_mean = sb("minus_mean", [P, T], F32)
        adj_in = sb("adj_in", [P, 2, N], I32)
        key = sb("key", [P, N], F32)
        top = sb("top", [P, 8 * ROUNDS], F32)
        index = sb("index", [P, 2, FIRST], I32)
        near = sb("near", [P, FIRST, D], F32)
        near_max = sb("near_max", [P, D], F32)
        mask_row = sb("mask_row", [P, N], BF16)
        peak = sb("peak", [P, 8], F32)
        minus_max = sb("minus_max", [P, 8], F32)
        total = sb("total", [P, 8], F32)
        inv_total = sb("inv_total", [P, 8], F32)
        s_now = sb("s_now", [P, D], F32)
        peak3 = sb("peak3", [P, 2], F32)
        minus_max3 = sb("minus_max3", [P, 2], F32)
        total3 = sb("total3", [P, 2], F32)
        inv_total3 = sb("inv_total3", [P, 2], F32)
        scaledT = U[:, 0, :].rearrange("p (q k i) -> p q k i", q=2, k=KINDS)
        kind_mask = U[:, 1:3, :].rearrange("p a n -> p (a n)").bitcast(U16).rearrange("p (k n) -> p k n", k=KINDS)
        aggT = W[:, 7, :]
        gelu_out = W[:, 0, :]
        probsT = [W[:, 4 + q, :].rearrange("p (t i) -> p t i", t=T) for q in range(2)]

        psA = psum("psA", [P, N], F32)
        psB = psum("psB", [P, N], F32)
        psC = psum("psC", [P, N], F32)
        acc = psum("acc", [P, N], F32)

        consts_loaded = sem("consts_loaded")
        all_x_loaded = sem("all_x_loaded")
        rows_stored = sem("rows_stored")
        graph_loaded = sem("graph_loaded")
        adj_in_loaded = [sem(f"adj_in_loaded{q}") for q in range(2)]
        out_stored = sem("out_stored")
        gathered = [sem(f"gathered{c}") for c in range(2)]
        zeroed = sem("zeroed")
        consts_made = sem("consts_made")
        weights_made = sem("weights_made")
        first_var = sem("first_var")
        first_std = sem("first_std")
        first_scale = sem("first_scale")
        first_h = sem("first_h")
        var_ready = sem("var_ready")
        std_ready = sem("std_ready")
        scale_ready = sem("scale_ready")
        h_ready = sem("h_ready")
        hT_ready = sem("hT_ready")
        adj_nat_ready = sem("adj_nat_ready")
        adj_turned_ready = sem("adj_turned_ready")
        adj_keyed = sem("adj_keyed")
        near_used = [sem(f"near_used{c}") for c in range(2)]
        index_ready = sem("index_ready")
        agg_ready = sem("agg_ready")
        aggT_ready = sem("aggT_ready")
        A_full, A_free = sem("A_full"), sem("A_free")
        B_full, B_free = sem("B_full"), sem("B_free")
        C_full, C_free = sem("C_full"), sem("C_free")
        O_full, O_free = sem("O_full"), sem("O_free")
        u_ready = sem("u_ready")
        su_ready = sem("su_ready")
        v_ready = sem("v_ready")
        s_ready = sem("s_ready")
        shift_ready = sem("shift_ready")
        row_probs = sem("row_probs")
        row_used = sem("row_used")
        s_scaled = sem("s_scaled")
        gelu_in_ready = sem("gelu_in_ready")
        gelu_ready = sem("gelu_ready")
        x_updated = sem("x_updated")
        left_scaled = sem("left_scaled")
        selected = sem("selected")
        probs3 = sem("probs3")
        probsT_ready = sem("probsT_ready")
        passed = sem("passed")

        block = ctx.enter_context(nc.Block())

        @block.sync
        def _(sp):
            a1_row = a1.rearrange("n c -> (c n)")
            loads = [
                (w0_own[:], W0[0:D, :]), (w0_agg[:], W0[D:2 * D, :]),
                (b0_row[:], b0.rearrange("(c n) -> c n", c=1)),
                (w1[:], W1), (a1_all[:], a1_row.partition_broadcast(P)),
                (w2[:], W2), (a2_all[:], a2.partition_broadcast(P)),
            ]
            loads += [(bias2_row[:], bias2.rearrange("(c n) -> c n", c=1))]
            loads += [(a3_cols[:, k:k + 1], a3[k]) for k in range(KINDS)]
            for b in range(B):
                sp.dma_start(W[:, b, :].rearrange("p (t f) -> p t f", t=T), x_view[b]).then_inc(all_x_loaded, 16)
            for dst, src in loads:
                sp.dma_start(dst, src).then_inc(consts_loaded, 16)

            def load_adj_tile(b, t):
                if not isinstance(b, int) or b * T + t >= 2:
                    sp.wait_ge(adj_keyed, b * T + (t - 1))
                    sp.wait_ge(adj_nat_ready, b * T + (t - 1))
                sp.dma_start(adj_in[:, t % 2, :], adj[b, t * P:(t + 1) * P, :]).then_inc(adj_in_loaded[t % 2], 16)

            load_adj_tile(0, 0)
            load_adj_tile(0, 1)
            sp.wait_ge(first_h, B)
            for b in range(B):
                sp.dma_start(hrows[b * STRIDE:b * STRIDE + N, :].rearrange("(t p) f -> p t f", p=P),
                             U[:, b, :].rearrange("p (t f) -> p t f", t=T)).then_inc(rows_stored, 16)
            sp.wait_ge(zeroed, 3)
            for b in range(B):
                sp.dma_start(hrows[b * STRIDE + N:(b + 1) * STRIDE, :], zeros[:]).then_inc(rows_stored, 16)
            for t in range(2, T):
                load_adj_tile(0, t)
            sp.wait_ge(rows_stored, 2 * B * 16)

            def graph(b, prep):
                sp.dma_start(xg[:], x_view[b]).then_inc(graph_loaded, 16)
                sp.dma_start(h[:], hrows[bass.ds(b * STRIDE, N), :].rearrange("(t p) f -> p t f", p=P))\
                    .then_inc(graph_loaded, 16)
                if prep:
                    for t in range(T):
                        load_adj_tile(b + 1, t)
                sp.wait_ge(x_updated, b * 4 + 4)
                sp.dma_start(out_view[b], xg[:]).then_inc(out_stored, 16)
                sp.wait_ge(out_stored, b * 16 + 16)
                sp.sem_inc(passed, 1)

            with sp.Fori(0, B - 1) as b:
                graph(b, True)
            graph(B - 1, False)

        @block.gpsimd
        def _(pool):
            nc.gpsimd.memset(identity[:], 0.0).then_inc(zeroed, 1)
            nc.gpsimd.memset(identity16[:], 0.0).then_inc(zeroed, 1)
            nc.gpsimd.memset(zeros[:], 0.0).then_inc(zeroed, 1)
            nc.gpsimd.memset(ones[:], 1.0).then_inc(consts_made, 1)
            pool.wait_ge(zeroed, 3)
            for m in (identity, identity16):
                nc.gpsimd.affine_select(out=m[:], in_=m[:], compare_op=ALU.not_equal, fill=1.0, base=0,
                                        pattern=[[-1, P]], channel_multiplier=1).then_inc(consts_made, 1)
            nc.gpsimd.iota(countdown[:], pattern=[[-1, N]], base=N, channel_multiplier=0,
                           allow_small_or_imprecise_dtypes=True).then_inc(consts_made, 1)
            nc.gpsimd.iota(row_base[:], pattern=[[STRIDE, B]], base=N, channel_multiplier=0,
                           allow_small_or_imprecise_dtypes=True).then_inc(consts_made, 1)
            pool.wait_ge(rows_stored, 2 * B * 16)
            for c in range(2):
                pool.sem_inc(near_used[c], 1)
            with pool.Fori(0, B * T // 2) as pair:
                for q in range(2):
                    n = pair * 2 + q
                    pool.wait_ge(index_ready, n + 1)
                    for c, part in enumerate(PARTS):
                        pool.wait_ge(near_used[c], n + 1)
                        pool.sem_inc(passed, 1)
                        for k in part:
                            nc.gpsimd.indirect_dma_start(
                                out=near[:, k, :], out_offset=None, in_=hrows,
                                in_offset=bass.IndirectOffsetOnAxis(ap=index[:, q, k:k + 1], axis=0)
                            ).then_inc(gathered[c], 16)

        @block.vector
        def _(dve):
            def norm_stats(xv, ready, made, count, scaled):
                for t in range(T):
                    nc.vector.bn_stats(stats[:, t, :], xv[:, t, :])
                dve.drain()
                for t in range(T):
                    nc.vector.bn_aggr(mean_var[:, t, :], stats[:, t, :])
                dve.drain()
                nc.vector.tensor_scalar(var_eps[:], mean_var[:, :, 1], EPS, None, ALU.add).then_inc(ready, 1)
                dve.wait_ge(made, count)
                nc.vector.reciprocal(rstd[:], std[:])
                dve.drain()
                nc.vector.scalar_tensor_tensor(out=minus_mean[:], in0=mean_var[:, :, 0], scalar=-1.0,
                                               in1=rstd[:], op0=ALU.mult, op1=ALU.mult).then_inc(scaled, 1)

            for b in range(B):
                dve.wait_ge(all_x_loaded, B * 16)
                if b:
                    dve.wait_ge(first_h, b)
                norm_stats(W[:, b, :].rearrange("p (t f) -> p t f", t=T), first_var, first_std, b + 1, first_scale)

            dve.wait_ge(consts_loaded, (8 + KINDS) * 16)
            dve.wait_ge(consts_made, 5)
            for col, a_part in ((w1_left, a1_all[:, 0:D]), (w1_right, a1_all[:, D:2 * D])):
                nc.vector.tensor_tensor(key[:, 0:D], w1[:], a_part, ALU.mult)
                dve.drain()
                nc.vector.reduce_sum(col[:], key[:, 0:D], AX.X)
                dve.drain()
            for cols, a_part in ((w2_left, a2_all[:, 0:HID]), (w2_right, a2_all[:, HID:2 * HID])):
                prod = key[:, 0:D].rearrange("p (h e) -> p h e", h=HEADS)
                for hd in range(HEADS):
                    nc.vector.tensor_tensor(prod[:, hd, :], w2[:, hd * HID:(hd + 1) * HID], a_part, ALU.mult)
                dve.drain()
                nc.vector.reduce_sum(cols[:], prod, AX.X)
                dve.drain()
            nc.vector.tensor_scalar(w1_left_rep[:], ones[:], w1_left[:, 0:1], None, ALU.mult)
            for hd in range(HEADS):
                nc.vector.tensor_scalar(w2_left_rep[:, hd, :], ones[:], w2_left[:, hd:hd + 1], None, ALU.mult)
            dve.drain()
            nc.vector.memset(peak[:], 0.0).then_inc(weights_made, 1)

            def neighbour_list(b, t, q):
                dve.wait_ge(adj_in_loaded[q], b * (16 * T // 2) + (t - q) * 8 + 16)
                dve.sem_inc(passed, 1)
                nc.vector.scalar_tensor_tensor(out=key[:], in0=adj_in[:, q, :], scalar=0.0, in1=countdown[:],
                                               op0=ALU.not_equal, op1=ALU.mult).then_inc(adj_keyed, 1)
                dve.drain()
                for r in range(ROUNDS):
                    nc.vector.max(out=top[:, 8 * r:8 * r + 8], in_=key[:])
                    dve.drain()
                    if r < ROUNDS - 1:
                        nc.vector.match_replace(out=key[:], in_to_replace=top[:, 8 * r:8 * r + 8],
                                                in_values=key[:], imm_value=0.0)
                        dve.drain()
                nc.vector.tensor_scalar(index[:, q, :], top[:, 0:FIRST], -1.0, row_base[:, bass.ds(b, 1)],
                                        ALU.mult, ALU.add).then_inc(index_ready, 1)

            def neighbour_max(b, t):
                row = agg[:, bass.ds(t, 1), :].rearrange("p a f -> p (a f)")
                dve.drain()
                for c, part in enumerate(PARTS):
                    size = len(part) * 16
                    dve.wait_ge(gathered[c], b * (T * size) + t * size + size)
                    nc.vector.reduce_max(row if c == 0 else near_max[:],
                                         near[:, part.start:part.stop, :].rearrange("p k f -> p f k"),
                                         AX.X).then_inc(near_used[c], 1)
                dve.drain()
                nc.vector.tensor_tensor(row, row, near_max[:], ALU.max).then_inc(agg_ready, 1)

            neighbour_list(0, 0, 0)
            for t in range(1, T):
                neighbour_list(0, t, t % 2)
                neighbour_max(0, t - 1)

            def normalise(b, layer):
                norm_stats(xg[:], var_ready, std_ready, b * 3 + layer, scale_ready)

            def leaky_scores(slot, hd, v_col):
                nc.vector.scalar_tensor_tensor(out=W[:, slot, :], in0=U[:, hd, :], scalar=v_col, in1=SU[:, hd, :],
                                               op0=ALU.add, op1=ALU.max)

            def mask_scores(slot, mask):
                nc.vector.tensor_tensor_reduce(out=W[:, slot, :], in0=W[:, slot, :], in1=mask, scale=1.0,
                                               scalar=LOWEST, op0=ALU.add, op1=ALU.max,
                                               accum_out=peak[:, slot:slot + 1])

            def shifts(lo):
                nc.vector.tensor_scalar(minus_max[:, lo:lo + 4], peak[:, lo:lo + 4], -1.0, None,
                                        ALU.mult).then_inc(shift_ready, 1)

            def update_x(src, b, layer):
                nc.vector.tensor_tensor(flat(xg[:]), src, flat(xg[:]), ALU.add).then_inc(x_updated, 1)

            def graph(b, prep):
                neighbour_max(b, T - 1)
                dve.wait_ge(graph_loaded, b * 32 + 32)
                dve.wait_ge(O_full, b * O_USES + O_L0 + 1)
                nc.vector.scalar_tensor_tensor(out=flat(xg[:]), in0=acc[:], scalar=0.0, in1=flat(xg[:]),
                                               op0=ALU.max, op1=ALU.add).then_inc(x_updated, 1)
                dve.wait_ge(x_updated, b * 4 + 1)
                dve.sem_inc(O_free, 1)

                normalise(b, 1)
                if prep:
                    neighbour_list(b + 1, 0, 0)
                    neighbour_list(b + 1, 1, 1)
                dve.wait_ge(adj_turned_ready, b * T + T)
                dve.wait_ge(u_ready, b * (1 + HEADS) + 1)
                dve.wait_ge(v_ready, b * 2 + 1)
                for g in range(2):
                    tiles = range(4 * g, 4 * g + 4)
                    for jt in tiles:
                        leaky_scores(jt, 0, V[:, jt, 0:1])
                    for jt in tiles:
                        dve.drain()
                        nc.vector.tensor_scalar(mask_row[:], adj_turned[:, jt, :], 0.0, NEG, ALU.is_le, ALU.mult)
                        dve.drain()
                        mask_scores(jt, mask_row[:])
                    dve.drain()
                    shifts(4 * g)
                dve.wait_ge(s_ready, b * 2 + 1)
                for g in range(2):
                    dve.wait_ge(row_probs, b * W_USES + 4 * g + 4)
                    nc.vector.reciprocal(inv_total[:, 4 * g:4 * g + 4], total[:, 4 * g:4 * g + 4])
                    dve.drain()
                    for jt in range(4 * g, 4 * g + 4):
                        last = nc.vector.tensor_scalar(s[:, jt, :], s[:, jt, :], inv_total[:, jt:jt + 1], None,
                                                       ALU.mult)
                    last.then_inc(s_scaled, 1)
                if prep:
                    neighbour_max(b + 1, 0)
                    neighbour_list(b + 1, 2, 0)
                dve.wait_ge(gelu_ready, b + 1)
                update_x(gelu_out, b, 1)
                dve.wait_ge(x_updated, b * 4 + 2)

                normalise(b, 2)
                if prep:
                    neighbour_max(b + 1, 1)
                    neighbour_list(b + 1, 3, 1)
                dve.wait_ge(v_ready, b * 2 + 2)
                dve.wait_ge(s_ready, b * 2 + 2)
                dve.wait_ge(u_ready, b * (1 + HEADS) + 1 + HEADS)

                def scale_s(jt, lo):
                    dve.wait_ge(row_probs, b * W_USES + jt * HEADS + (8 + lo + 4))
                    nc.vector.reciprocal(inv_total[:, lo:lo + 4], total[:, lo:lo + 4])
                    dve.drain()
                    cols = slice(lo * HID, (lo + 4) * HID)
                    nc.vector.tensor_tensor(
                        s_now[:, cols].rearrange("p (h e) -> p h e", h=4),
                        s[:, bass.ds(jt, 1), cols].rearrange("p a (h e) -> p (a h) e", h=4),
                        inv_total[:, lo:lo + 4].unsqueeze(2).to_broadcast([P, 4, HID]), ALU.mult).then_inc(s_scaled, 1)

                def score_tiles(quad, more):
                    before = None
                    for c in range(4):
                        jt = quad * 4 + c
                        for lo in (0, 4):
                            if lo == 0:
                                nc.vector.tensor_scalar(mask_row[:], adj_turned[:, bass.ds(jt, 1), :].rearrange("p a n -> p (a n)"),
                                                        0.0, NEG, ALU.is_equal, ALU.mult)
                            for hd in range(lo, lo + 4):
                                dve.wait_ge(row_used, b * W_USES + jt * HEADS + (hd + 1))
                                leaky_scores(hd, hd, V[:, bass.ds(jt, 1), hd:hd + 1].rearrange("p a e -> p (a e)"))
                            if before:
                                scale_s(*before)
                            before = (jt, lo)
                            dve.drain()
                            for hd in range(lo, lo + 4):
                                mask_scores(hd, mask_row[:])
                            dve.drain()
                            shifts(lo)
                        if c % 2 == 0:
                            more(quad * 2 + c // 2, c // 2)
                    scale_s(*before)

                def next_lists(n, q):
                    if prep:
                        neighbour_max(b + 1, n + 2)
                        neighbour_list(b + 1, n + 4, q)

                dve.sem_inc(passed, 1)
                with dve.Fori(0, T // 4) as quad:
                    score_tiles(quad, next_lists)
                dve.wait_ge(O_full, b * O_USES + O_L2 + 1)
                update_x(acc[:], b, 2)
                dve.wait_ge(x_updated, b * 4 + 3)
                dve.sem_inc(O_free, 1)

                normalise(b, 3)
                if prep:
                    neighbour_max(b + 1, T - 2)
                dve.wait_ge(hT_ready, b * 4 + 4)

                def scale_left(it, q):
                    dve.wait_ge(B_full, b * B_USES + it * 2 + (B_L3 - 2))
                    for k in range(KINDS):
                        last = nc.vector.tensor_scalar(scaledT[:, q, k, :], hT[:, bass.ds(it * P, P)],
                                                       a3_cols[:, k:k + 1], None, ALU.mult)
                    last.then_inc(left_scaled, 1)

                def select(it, q):
                    nat = adj_nat[:, bass.ds(b % 2, 1), bass.ds(it, 1), :].rearrange("p c a n -> p (c a n)")
                    dve.wait_ge(C_full, b * C_USES + it + (C_L3 - 1))
                    nc.vector.tensor_scalar(mask_row[:], nat, 1.0, NEG, ALU.not_equal, ALU.mult)
                    for k in range(1, KINDS):
                        nc.vector.tensor_scalar(kind_mask[:, k, :], nat, k + 1.0, None, ALU.is_equal)
                    dve.drain()
                    for k in range(KINDS):
                        full, free, ps = ((A_full, A_free, psA), (B_full, B_free, psB))[k % 2]
                        base = b * (A_USES, B_USES)[k % 2] + it * 2 + ((A_L3, B_L3)[k % 2] + k // 2 + 1)
                        dve.wait_ge(full, base)
                        if k == 0:
                            nc.vector.tensor_tensor(W[:, q, :], ps[:], mask_row[:], ALU.add).then_inc(free, 1)
                        else:
                            dve.sem_inc(passed, 1)
                            nc.vector.copy_predicated(W[:, q, :], kind_mask[:, k, :], ps[:]).then_inc(free, 1)
                        dve.drain()
                    nc.vector.scalar_tensor_tensor(out=W[:, q, :], in0=W[:, q, :], scalar=SLOPE3, in1=W[:, q, :],
                                                   op0=ALU.mult, op1=ALU.max)
                    dve.drain()
                    nc.vector.reduce_max(peak3[:, q:q + 1], W[:, q, :], AX.X)
                    dve.drain()
                    nc.vector.tensor_scalar(minus_max3[:, q:q + 1], peak3[:, q:q + 1], -1.0, None,
                                            ALU.mult).then_inc(selected, 1)

                def finish_rows(it, q):
                    dve.wait_ge(probs3, b * T + it + 1)
                    nc.vector.reciprocal(inv_total3[:, q:q + 1], total3[:, q:q + 1])
                    dve.drain()
                    dve.wait_ge(O_full, b * O_USES + it + (O_L3 + 1))
                    xt = xg[:, bass.ds(it, 1), :].rearrange("p a f -> p (a f)")
                    nc.vector.scalar_tensor_tensor(out=xt, in0=acc[:, q * HALF:q * HALF + D], scalar=inv_total3[:, q:q + 1],
                                                   in1=xt, op0=ALU.mult, op1=ALU.add).then_inc(O_free, 1)

                scale_left(0, 0)
                scale_left(1, 1)
                select(0, 0)
                with dve.Fori(0, T // 2 - 1) as pair:
                    it = pair * 2
                    scale_left(it + 2, 0)
                    select(it + 1, 1)
                    finish_rows(it, 0)
                    scale_left(it + 3, 1)
                    select(it + 2, 0)
                    finish_rows(it + 1, 1)
                select(T - 1, 1)
                finish_rows(T - 2, 0)
                finish_rows(T - 1, 1)
                dve.drain()
                nc.vector.memset(peak[:, 0:1], 0.0).then_inc(x_updated, 1)

            with dve.Fori(0, B - 1) as b:
                graph(b, True)
            graph(B - 1, False)

        @block.scalar
        def _(act):
            for b in range(B):
                act.wait_ge(first_var, b + 1)
                nc.scalar.activation(std[:], var_eps[:], ACT.Sqrt).then_inc(first_std, 1)
                act.wait_ge(first_scale, b + 1)
                for t in range(T):
                    last = nc.scalar.activation(U[:, b, t * D:(t + 1) * D], W[:, b, t * D:(t + 1) * D], ACT.Relu,
                                                bias=minus_mean[:, t:t + 1], scale=rstd[:, t:t + 1])
                last.then_inc(first_h, 1)

            def take_adj(b, t, q):
                act.wait_ge(adj_in_loaded[q], b * (16 * T // 2) + (t - q) * 8 + 16)
                dst = adj_nat[:, bass.ds(b % 2, 1), bass.ds(t, 1), :].rearrange("p c a n -> p (c a n)")
                nc.scalar.copy(dst, adj_in[:, q, :]).then_inc(adj_nat_ready, 1)

            for t in range(T):
                take_adj(0, t, t % 2)

            def graph(b, prep):
                def turn(full, count, src, dst, free, ready, ready_count):
                    act.wait_ge(full, count)
                    nc.scalar.copy(dst, src).then_inc(ready, 1)
                    act.wait_ge(ready, ready_count)
                    act.sem_inc(free, 1)

                turn(A_full, b * A_USES + A_H0 + 1, psA[:], hT[:], A_free, hT_ready, b * 4 + 1)
                turn(B_full, b * B_USES + B_AGG + 1, psB[:], aggT, B_free, aggT_ready, b + 1)
                for jt in range(T):
                    ps, full, free, uses, first = ((psB, B_full, B_free, B_USES, B_ADJ),
                                                   (psC, C_full, C_free, C_USES, C_ADJ))[jt % 2]
                    turn(full, b * uses + first + jt // 2 + 1, ps[:], adj_turned[:, jt, :], free,
                         adj_turned_ready, b * T + jt + 1)

                def normalise(layer, a_use):
                    act.wait_ge(var_ready, b * 3 + layer)
                    nc.scalar.activation(std[:], var_eps[:], ACT.Sqrt).then_inc(std_ready, 1)
                    act.wait_ge(scale_ready, b * 3 + layer)
                    for t in range(T):
                        last = nc.scalar.activation(h[:, t, :], xg[:, t, :], ACT.Relu, bias=minus_mean[:, t:t + 1],
                                                    scale=rstd[:, t:t + 1])
                    last.then_inc(h_ready, 1)
                    turn(A_full, b * A_USES + a_use + 1, psA[:], hT[:], A_free, hT_ready, b * 4 + layer + 1)

                def probabilities(group, lo):
                    act.wait_ge(shift_ready, b * G_USES + group)
                    for q in range(lo, lo + 4):
                        nc.scalar.activation(W[:, q, :], W[:, q, :], ACT.Exp, bias=minus_max[:, q:q + 1],
                                             accum_out=total[:, q:q + 1]).then_inc(row_probs, 1)

                def turn_scores(full, count, ps, hd, free, slope, n):
                    act.wait_ge(full, count)
                    nc.scalar.mul(SU[:, hd, :], ps[:], slope).then_inc(su_ready, 1)
                    act.wait_ge(su_ready, b * (1 + HEADS) + n)
                    turn(full, count, ps[:], U[:, hd, :], free, u_ready, b * (1 + HEADS) + n)

                def turn_right(count, src, dst, slope):
                    act.wait_ge(O_full, count)
                    nc.scalar.mul(dst, src, 1.0 - slope).then_inc(v_ready, 1)

                normalise(1, A_H1)
                turn_scores(B_full, b * B_USES + B_U1 + 1, psB, 0, B_free, SLOPE1, 1)
                turn(C_full, b * C_USES + C_S1 + 1, psC[:], flat(s[:]), C_free, s_ready, b * 2 + 1)
                turn_right(b * O_USES + O_V1 + 1, acc[:, 0:T], V[:, :, 0], SLOPE1)
                act.wait_ge(v_ready, b * 2 + 1)
                act.sem_inc(O_free, 1)
                if prep:
                    take_adj(b + 1, 0, 0)
                    take_adj(b + 1, 1, 1)
                probabilities(1, 0)
                probabilities(2, 4)
                if prep:
                    take_adj(b + 1, 2, 0)
                turn(O_full, b * O_USES + O_L1 + 1, acc[:], W[:, 1, :], O_free, gelu_in_ready, b + 1)
                nc.scalar.activation(gelu_out, W[:, 1, :], ACT.Gelu).then_inc(gelu_ready, 1)

                normalise(2, A_H2)
                for hd in range(HEADS):
                    ps, full, free, count = ((psB, B_full, B_free, b * B_USES + B_U2 + (hd // 2 + 1)),
                                             (psC, C_full, C_free, b * C_USES + C_U2 + (hd // 2 + 1)))[hd % 2]
                    turn_scores(full, count, ps, hd, free, SLOPE2, hd + 2)
                turn(A_full, b * A_USES + A_S2 + 1, psA[:], flat(s[:]), A_free, s_ready, b * 2 + 2)
                turn_right(b * O_USES + O_V2 + 1, acc[:, 0:T * HEADS], V[:].rearrange("p t h -> p (t h)"), SLOPE2)
                act.wait_ge(v_ready, b * 2 + 2)
                act.sem_inc(O_free, 1)
                if prep:
                    take_adj(b + 1, 3, 1)
                with act.Fori(0, T // 4) as quad:
                    for c in range(4):
                        group = quad * 8 + (2 * c + 3)
                        probabilities(group, 0)
                        probabilities(group + 1, 4)
                        if prep and c % 2 == 0:
                            take_adj(b + 1, quad * 2 + (4 + c // 2), c // 2)

                normalise(3, A_H3)
                with act.Fori(0, T // 2) as pair:
                    for q in range(2):
                        it = pair * 2 + q
                        act.wait_ge(selected, b * T + it + 1)
                        nc.scalar.activation(W[:, q, :], W[:, q, :], ACT.Exp, bias=minus_max3[:, q:q + 1],
                                             accum_out=total3[:, q:q + 1]).then_inc(probs3, 1)
                        act.wait_ge(O_full, b * O_USES + it + (O_L3 - 1))
                        turn(C_full, b * C_USES + it + (C_L3 + 1), psC[:], flat(probsT[q]), C_free, probsT_ready,
                             b * T + it + 1)
                act.wait_ge(x_updated, b * 4 + 4)

            with act.Fori(0, B - 1) as b:
                graph(b, True)
            graph(B - 1, False)

        @block.tensor
        def _(pe):
            for free in (A_free, B_free, C_free, O_free):
                pe.sem_inc(free, 1)
            pe.wait_ge(consts_made, 5)
            pe.wait_ge(weights_made, 1)
            pe.wait_ge(consts_loaded, (8 + KINDS) * 16)

            def mm(dst, lhsT, rhs, start=True, stop=True):
                return nc.tensor.matmul(dst, lhsT, rhs, start=start, stop=stop, skip_group_check=True)

            def turn_tiles(dst, src, full):
                for t in range(T):
                    last = nc.tensor.transpose(dst[:, t * P:(t + 1) * P], src(t), identity[:])
                last.then_inc(full, 1)

            def graph(b):
                pe.wait_ge(graph_loaded, b * 32 + 32)
                pe.wait_ge(A_free, b * A_USES + A_H0 + 1)
                turn_tiles(psA, lambda t: h[:, t, :], A_full)
                pe.wait_ge(agg_ready, b * T + T)
                pe.wait_ge(B_free, b * B_USES + B_AGG + 1)
                turn_tiles(psB, lambda t: agg[:, t, :], B_full)
                pe.wait_ge(hT_ready, b * 4 + 1)
                pe.wait_ge(aggT_ready, b + 1)
                pe.wait_ge(O_free, b * O_USES + O_L0 + 1)
                for t in range(T):
                    dst = acc[:, t * D:(t + 1) * D]
                    mm(dst, hT[:, t * P:(t + 1) * P], w0_own[:], True, False)
                    mm(dst, aggT[:, t * P:(t + 1) * P], w0_agg[:], False, False)
                    last = mm(dst, ones[0:1, :], b0_row[:], False, True)
                last.then_inc(O_full, 1)
                pe.wait_ge(adj_nat_ready, b * T + T)
                for jt in range(T):
                    ps, full, free, uses, first = ((psB, B_full, B_free, B_USES, B_ADJ),
                                                   (psC, C_full, C_free, C_USES, C_ADJ))[jt % 2]
                    pe.wait_ge(free, b * uses + (first + jt // 2 + 1))
                    for it in range(T):
                        tile = adj_nat[:, bass.ds(b % 2, 1), it, jt * P:(jt + 1) * P].rearrange("p c n -> p (c n)")
                        last = mm(ps[:, it * P:(it + 1) * P], tile, identity16[:])
                    last.then_inc(full, 1)

                def turn_h(layer, a_use):
                    pe.wait_ge(h_ready, b * 3 + layer)
                    pe.wait_ge(A_free, b * A_USES + a_use + 1)
                    turn_tiles(psA, lambda t: h[:, t, :], A_full)
                    pe.wait_ge(hT_ready, b * 4 + layer + 1)

                def spread(ps, rep, full):
                    for c in range(2):
                        last = mm(ps[:, c * HALF:(c + 1) * HALF], rep, hT[:, c * HALF:(c + 1) * HALF])
                    last.then_inc(full, 1)

                def start_sums(row):
                    for t in range(T):
                        mm(acc[:, t * D:(t + 1) * D], ones[0:1, :], row, t * D % HALF == 0, False)

                def project(ps, weight, full):
                    n = weight.shape[1]
                    for t in range(T):
                        last = mm(ps[:, t * n:(t + 1) * n], hT[:, t * P:(t + 1) * P], weight)
                    last.then_inc(full, 1)

                turn_h(1, A_H1)
                pe.wait_ge(B_free, b * B_USES + B_U1 + 1)
                spread(psB, w1_left_rep[:], B_full)
                pe.wait_ge(C_free, b * C_USES + C_S1 + 1)
                project(psC, w1[:], C_full)
                pe.wait_ge(O_free, b * O_USES + O_V1 + 1)
                project(acc, w1_right[:], O_full)
                pe.wait_ge(O_free, b * O_USES + O_L1 + 1)
                start_sums(zeros[0:1, :])
                for g in range(2):
                    pe.wait_ge(s_scaled, b * G_USES + (g + 1))
                    for jt in range(4 * g, 4 * g + 4):
                        for it in range(T):
                            last = mm(acc[:, it * D:(it + 1) * D], W[:, jt, it * P:(it + 1) * P], s[:, jt, :],
                                      False, False)
                last.then_inc(O_full, 1)

                turn_h(2, A_H2)
                for hd in range(HEADS):
                    ps, full, free, count = ((psB, B_full, B_free, b * B_USES + B_U2 + (hd // 2 + 1)),
                                             (psC, C_full, C_free, b * C_USES + C_U2 + (hd // 2 + 1)))[hd % 2]
                    pe.wait_ge(free, count)
                    spread(ps, w2_left_rep[:, hd, :], full)
                pe.wait_ge(A_free, b * A_USES + A_S2 + 1)
                project(psA, w2[:], A_full)
                pe.wait_ge(O_free, b * O_USES + O_V2 + 1)
                project(acc, w2_right[:], O_full)
                pe.wait_ge(gelu_ready, b + 1)
                pe.sem_inc(row_used, 8)
                pe.wait_ge(O_free, b * O_USES + O_L2 + 1)
                start_sums(bias2_row[:])
                with pe.Fori(0, T) as jt:
                    for lo in (0, 4):
                        pe.wait_ge(s_scaled, b * G_USES + jt * 2 + (3 + lo // 4))
                        for hd in range(lo, lo + 4):
                            for it in range(T):
                                at = it * D + hd * HID
                                last = mm(acc[:, at:at + HID], W[:, hd, it * P:(it + 1) * P],
                                          s_now[:, hd * HID:(hd + 1) * HID], False, False)
                            last.then_inc(row_used, 1)
                pe.wait_ge(row_used, b * W_USES + W_USES)
                pe.sem_inc(O_full, 1)

                turn_h(3, A_H3)

                def scores(it, q):
                    pe.wait_ge(left_scaled, b * T + it + 1)
                    for k in range(KINDS):
                        ps, full, free, uses, first = ((psA, A_full, A_free, A_USES, A_L3),
                                                       (psB, B_full, B_free, B_USES, B_L3))[k % 2]
                        pe.wait_ge(free, b * uses + it * 2 + (first + k // 2 + 1))
                        spread(ps, scaledT[:, q, k, :], full)

                def combine(it, q):
                    pe.wait_ge(probs3, b * T + it + 1)
                    pe.wait_ge(C_free, b * C_USES + it + (C_L3 + 1))
                    turn_tiles(psC, lambda t: W[:, q, t * P:(t + 1) * P], C_full)
                    pe.wait_ge(probsT_ready, b * T + it + 1)
                    pe.wait_ge(O_free, b * O_USES + it + O_L3)
                    for jt in range(T):
                        last = mm(acc[:, q * HALF:q * HALF + D], probsT[q][:, jt, :], h[:, jt, :], jt == 0, jt == T - 1)
                    last.then_inc(O_full, 1)

                scores(0, 0)
                with pe.Fori(0, T // 2 - 1) as pair:
                    it = pair * 2
                    scores(it + 1, 1)
                    combine(it, 0)
                    scores(it + 2, 0)
                    combine(it + 1, 1)
                scores(T - 1, 1)
                combine(T - 2, 0)
                combine(T - 1, 1)

            with pe.Fori(0, B) as b:
                graph(b)


_INS = ['x', 'adj', 'L0_gnn_W', 'L0_gnn_b', 'L1_gnn_W', 'L1_gnn_a', 'L2_gnn_W', 'L2_gnn_a', 'L2_gnn_bias',
        'L3_gnn_a_0', 'L3_gnn_a_1', 'L3_gnn_a_2', 'L3_gnn_a_3']


def kernel(**inputs):
    import numpy as _np
    import concourse.bacc as _bacc
    from concourse.bass_utils import run_bass_kernel_spmd as _run

    nc = _bacc.Bacc("TRN2", target_bir_lowering=False, num_devices=1)
    arrays, args = {}, []
    for name in _INS:
        a = _np.ascontiguousarray(inputs[name])
        arrays[f"in_{name}_dram"] = a
        args.append(nc.dram_tensor(f"in_{name}_dram", a.shape, mybir.dt.from_np(a.dtype), kind="ExternalInput").ap())
    out = nc.dram_tensor("out_0_dram", inputs['x'].shape, F32, kind="ExternalOutput").ap()
    graph_layers(nc, *args[:9], args[9:], out)
    r = _run(nc, [arrays], core_ids=[0])
    return r.results[0]["out_0_dram"]
```

```python
from contextlib import ExitStack

import concourse.bass as bass
from concourse import mybir

ALU = mybir.AluOpType
ACT = mybir.ActivationFunctionType
AX = mybir.AxisListType
F32 = mybir.dt.float32
BF16 = mybir.dt.bfloat16
I32 = mybir.dt.int32
U16 = mybir.dt.uint16

P = 128
EPS = 1e-5
FIRST = 25
HEADS = 8
KINDS = 4
NEG = -float(2 ** 66)
LOWEST = -3.0e38
SLOPE1, SLOPE2, SLOPE3 = 0.4, 0.2, 0.2
PAD = 16


def graph_layers(nc, x, adj, W0, b0, W1, a1, W2, a2, bias2, a3, out):
    B, N, D = x.shape
    T = N // P
    HALF = N // 2
    HID = D // HEADS
    STRIDE = N + PAD
    ROUNDS = -(-FIRST // 8)
    PARTS = (range(0, 8), range(8, 16), range(16, FIRST))
    LAST = len(PARTS) - 1

    LOADS = 7 + HEADS + KINDS
    QUAD = 4
    ROWS = T + HEADS * T
    GROUPS = ROWS // QUAD
    GROUPS2 = HEADS * T // QUAD
    SLOTS = 2 * HEADS

    A_H0, A_H1, A_PARTS1, A_MASK1, A_H2, A_PARTS2 = 0, 1, 2, 3, 3 + T // 2, 4 + T // 2
    A_S2, A_MASK2 = A_PARTS2 + 1, A_PARTS2 + 2
    A_BACK = A_MASK2 + HEADS * T // 2
    A_H3, A_L3 = A_BACK + 1, A_BACK + 2
    A_USES = A_L3 + 2 * T
    B_AGG, B_U1, B_MASK1 = 1, 1 + T // 2, 2 + T // 2
    B_U2 = B_MASK1 + T // 2
    B_MASK2 = B_U2 + HEADS // 2
    B_BACK = B_MASK2 + HEADS * T // 2
    B_L3 = B_BACK + 1
    B_USES = B_L3 + 2 * T
    C_VALUES, C_S1 = 2, T // 2 + 1
    C_U2 = C_S1 + 1
    C_L2 = C_U2 + HEADS // 2
    C_L3 = C_L2 + 1
    C_USES = C_L3 + T
    O_L0, O_V1, O_L1, O_V2, O_L2, O_L3 = range(6)
    O_USES = O_L3 + T

    hrows = nc.dram_tensor("hrows", [B * STRIDE, D], F32, kind="Internal").ap()
    x_view = x.rearrange("b (t p) f -> b p t f", p=P)
    out_view = out.rearrange("b (t p) f -> b p t f", p=P)

    def adj_use(jt):
        return jt // 2 + (jt % 2 == 0 and jt > 0) + (jt % 2 == 1 and jt > 3)

    def flat(ap):
        return ap.rearrange("p a f -> p (a f)")

    with ExitStack() as ctx:
        def sb(name, shape, dt):
            return ctx.enter_context(nc.sbuf_tensor(name, shape, dt))

        def psum(name, shape, dt):
            return ctx.enter_context(nc.psum_tensor(name, shape, dt))

        def sem(name):
            return ctx.enter_context(nc.semaphore(name))

        identity = sb("identity", [P, P], F32)
        identity16 = sb("identity16", [P, P], BF16)
        ones = sb("ones", [P, P], F32)
        ones16 = sb("ones16", [P, 1], BF16)
        zeros = sb("zeros", [PAD, D], F32)
        countdown = sb("countdown", [P, N], U16)
        row_base = sb("row_base", [P, B], F32)
        w0_own = sb("w0_own", [D, D], F32)
        w0_agg = sb("w0_agg", [D, D], F32)
        b0_row = sb("b0_row", [1, D], F32)
        w1 = sb("w1", [D, D], F32)
        w2 = sb("w2", [D, D], F32)
        bias2_cols = sb("bias2_cols", [P, 2], F32)
        a3_cols = sb("a3_cols", [D, KINDS], F32)
        w1_a = sb("w1_a", [D, 2], F32)
        w2_a = sb("w2_a", [D, 2 * HEADS], F32)
        pick = sb("pick", [96, HEADS, P], BF16)

        xg = sb("xg", [P, T, D], F32)
        h = sb("h", [P, T, D], F32)
        hT = sb("hT", [D, N], F32)
        s = sb("s", [P, T, D], F32)
        adj_nat = sb("adj_nat", [P, 2, T, N], BF16)
        adj_turned = sb("adj_turned", [P, T, N], BF16)
        agg = sb("agg", [P, T, D], F32)
        U = sb("U", [P, HEADS, N], F32)
        W = sb("W", [P, SLOTS, N], F32)
        V = sb("V", [P, T, HEADS], F32)

        stats = sb("stats", [P, T, 6], F32)
        mean_var = sb("mean_var", [P, T, 2], F32)
        var_eps = sb("var_eps", [P, T], F32)
        std = sb("std", [P, T], F32)
        rstd = sb("rstd", [P, T], F32)
        minus_mean = sb("minus_mean", [P, T], F32)
        adj_in = sb("adj_in", [P, 2, N], I32)
        key = sb("key", [P, N], F32)
        top = sb("top", [P, 8 * ROUNDS], F32)
        index = sb("index", [P, 2, FIRST], I32)
        near = sb("near", [P, FIRST, D], F32)
        near_max = sb("near_max", [P, D], F32)
        mask_rows = sb("mask_rows", [P, 2, N], BF16)
        mask_row = mask_rows[:, 0, :]
        su = sb("su", [P, T, HEADS], F32)
        rest = sb("rest", [P, T, HEADS], F32)
        parts = sb("parts", [P, T, 96], BF16)
        part_rows = sb("part_rows", [96, N], BF16)
        peak = sb("peak", [P, 8], F32)
        minus_max = sb("minus_max", [P, 8], F32)
        total = sb("total", [P, 8], F32)
        inv_total = sb("inv_total", [P, 8], F32)
        a1_all = agg[:, 0:2, :].rearrange("p a f -> p (a f)")
        a2_all = agg[:, 2, 0:2 * HID]
        s_now = sb("s_now", [P, D], F32)
        peak3 = sb("peak3", [P, 2], F32)
        minus_max3 = sb("minus_max3", [P, 2], F32)
        total3 = sb("total3", [P, 2], F32)
        inv_total3 = sb("inv_total3", [P, 2], F32)
        squares = sb("squares", [P, 1], F32)
        beyond = sb("beyond", [P, 2], F32)
        is_long = sb("is_long", [1, 1], F32)
        long_sum = sb("long_sum", [1, 1], F32)
        long_lists = sb("long_lists", [1, T], I32)
        long_sums = sb("long_sums", [1, T], I32)
        many_kinds = sb("many_kinds", [1, 1], I32)
        scaledT = U[:, 0, :].rearrange("p (q k i) -> p q k i", q=2, k=KINDS)
        kind_mask = U[:, 1:3, :].rearrange("p a n -> p (a n)").bitcast(U16).rearrange("p (k n) -> p k n", k=KINDS)
        aggT = W[:, 7, :]
        gelu_out = W[:, 0, :]
        sums_turned = [W[:, 8 + q, :] for q in range(2)]
        probsT = [W[:, 4 + q, :].rearrange("p (t i) -> p t i", t=T) for q in range(2)]

        psA = psum("psA", [P, N], F32)
        psB = psum("psB", [P, N], F32)
        psC = psum("psC", [P, N], F32)
        acc = psum("acc", [P, N], F32)

        consts_loaded = sem("consts_loaded")
        first_x_loaded = sem("first_x_loaded")
        other_x_loaded = sem("other_x_loaded")
        first_rows_stored = sem("first_rows_stored")
        other_rows_stored = sem("other_rows_stored")
        x_loaded = sem("x_loaded")
        h_loaded = sem("h_loaded")
        adj_in_loaded = [sem(f"adj_in_loaded{q}") for q in range(2)]
        out_stored = sem("out_stored")
        gathered = [sem(f"gathered{c}") for c in range(LAST + 1)]
        first_gathered = sem("first_gathered")
        zeroed = sem("zeroed")
        consts_made = sem("consts_made")
        cleared = sem("cleared")
        weights_made = sem("weights_made")
        first_var = sem("first_var")
        first_std = sem("first_std")
        first_scale = sem("first_scale")
        first_h = sem("first_h")
        var_ready = sem("var_ready")
        std_ready = sem("std_ready")
        scale_ready = sem("scale_ready")
        h_ready = sem("h_ready")
        hT_ready = sem("hT_ready")
        adj_nat_ready = sem("adj_nat_ready")
        adj_turned_ready = sem("adj_turned_ready")
        adj_keyed = sem("adj_keyed")
        near_used = [sem(f"near_used{c}") for c in range(LAST + 1)]
        index_ready = sem("index_ready")
        round_ready = sem("round_ready")
        long_summed = sem("long_summed")
        long_ready = sem("long_ready")
        agg_ready = sem("agg_ready")
        aggT_ready = sem("aggT_ready")
        A_full, A_free = sem("A_full"), sem("A_free")
        B_full, B_free = sem("B_full"), sem("B_free")
        C_full, C_free = sem("C_full"), sem("C_free")
        O_full, O_free = sem("O_full"), sem("O_free")
        parts_ready = sem("parts_ready")
        part_rows_ready = sem("part_rows_ready")
        u_ready = sem("u_ready")
        masks_ready = sem("masks_ready")
        row_relu = sem("row_relu")
        sums_ready = sem("sums_ready")
        v_ready = sem("v_ready")
        s_ready = sem("s_ready")
        shift_ready = sem("shift_ready")
        row_probs = sem("row_probs")
        row_used = sem("row_used")
        s_scaled = sem("s_scaled")
        gelu_ready = sem("gelu_ready")
        x_updated = sem("x_updated")
        left_scaled = sem("left_scaled")
        values_summed = sem("values_summed")
        beyond_ready = sem("beyond_ready")
        many_kinds_ready = sem("many_kinds_ready")
        relu3 = sem("relu3")
        selected = sem("selected")
        probs3 = sem("probs3")
        probsT_ready = sem("probsT_ready")
        passed = sem("passed")

        block = ctx.enter_context(nc.Block())

        @block.sync
        def _(sp):
            a1_row = a1.rearrange("n c -> (c n)")
            loads = [
                (w0_own[:], W0[0:D, :]), (w0_agg[:], W0[D:2 * D, :]),
                (b0_row[:], b0.rearrange("(c n) -> c n", c=1)),
                (w1[:], W1), (a1_all, a1_row.partition_broadcast(P)),
                (w2[:], W2), (a2_all, a2.partition_broadcast(P)),
            ]
            loads += [(bias2_cols[32 * (hd % QUAD):32 * (hd % QUAD) + HID, hd // QUAD:hd // QUAD + 1],
                       bias2.rearrange("(n c) -> n c", c=1)[hd * HID:(hd + 1) * HID, :]) for hd in range(HEADS)]
            loads += [(a3_cols[:, k:k + 1], a3[k]) for k in range(KINDS)]
            def load_adj_tile(b, t):
                if not isinstance(b, int) or b * T + t >= 2:
                    sp.wait_ge(adj_keyed, b * T + (t - 1))
                    sp.wait_ge(adj_nat_ready, b * T + (t - 1))
                sp.dma_start(adj_in[:, t % 2, :], adj[b, t * P:(t + 1) * P, :]).then_inc(adj_in_loaded[t % 2], 16)

            def stage_x(b, loaded):
                sp.dma_start(W[:, b, :].rearrange("p (t f) -> p t f", t=T), x_view[b]).then_inc(loaded, 16)

            def store_rows(b, stored):
                sp.wait_ge(first_h, b + 1)
                sp.dma_start(hrows[b * STRIDE:b * STRIDE + N, :].rearrange("(t p) f -> p t f", p=P),
                             U[:, b, :].rearrange("p (t f) -> p t f", t=T)).then_inc(stored, 16)

            stage_x(0, first_x_loaded)
            load_adj_tile(0, 0)
            load_adj_tile(0, 1)
            sp.wait_ge(cleared, 2)
            for dst, src in loads:
                sp.dma_start(dst, src).then_inc(consts_loaded, 16)
            for b in range(1, B):
                stage_x(b, other_x_loaded)
            store_rows(0, first_rows_stored)
            sp.wait_ge(zeroed, 3)
            for b in range(B):
                sp.dma_start(hrows[b * STRIDE + N:(b + 1) * STRIDE, :], zeros[:]).then_inc(first_rows_stored, 16)
            for t in range(2, T):
                load_adj_tile(0, t)
                store_rows(t - 1, other_rows_stored)
            for b in range(T - 1, B):
                store_rows(b, other_rows_stored)
            sp.wait_ge(first_rows_stored, (1 + B) * 16)
            sp.wait_ge(other_rows_stored, (B - 1) * 16)

            def load_x(b):
                sp.dma_start(xg[:], x_view[b]).then_inc(x_loaded, 16)

            def load_h(b):
                sp.dma_start(h[:], hrows[bass.ds(b * STRIDE, N), :].rearrange("(t p) f -> p t f", p=P))\
                    .then_inc(h_loaded, 16)

            def graph(b, prep):
                if prep:
                    load_adj_tile(b + 1, 0)
                    load_adj_tile(b + 1, 1)
                sp.wait_ge(out_stored, b * 16 + 1)
                sp.sem_inc(passed, 1)
                load_x(b)
                if prep:
                    for t in range(2, T):
                        load_adj_tile(b + 1, t)
                    sp.wait_ge(O_full, b * O_USES + O_USES)
                    sp.sem_inc(passed, 1)
                    load_h(b + 1)

            load_h(0)
            sp.sem_inc(out_stored, 1)
            with sp.Fori(0, B - 1) as b:
                graph(b, True)
            graph(B - 1, False)
            sp.wait_ge(out_stored, B * 16 + 1)

        @block.gpsimd
        def _(pool):
            nc.gpsimd.memset(identity[:], 0.0).then_inc(zeroed, 1)
            nc.gpsimd.memset(identity16[:], 0.0).then_inc(zeroed, 1)
            nc.gpsimd.memset(zeros[:], 0.0).then_inc(zeroed, 1)
            nc.gpsimd.memset(ones[:], 1.0).then_inc(consts_made, 1)
            nc.gpsimd.memset(ones16[:], 1.0).then_inc(consts_made, 1)
            pool.wait_ge(zeroed, 3)
            for m in (identity, identity16):
                nc.gpsimd.affine_select(out=m[:], in_=m[:], compare_op=ALU.not_equal, fill=1.0, base=0,
                                        pattern=[[-1, P]], channel_multiplier=1).then_inc(consts_made, 1)
            nc.gpsimd.memset(bias2_cols[:], 0.0).then_inc(cleared, 1)
            nc.gpsimd.memset(parts[:], 0.0).then_inc(cleared, 1)
            nc.gpsimd.memset(pick[:], 0.0).then_inc(zeroed, 1)
            pool.wait_ge(zeroed, 4)
            for part in range(3):
                pool.wait_ge(consts_made, 4 + part)
                rows = pick[32 * part:32 * part + HEADS, :, :]
                nc.gpsimd.affine_select(out=rows, in_=rows, compare_op=ALU.not_equal, fill=1.0, base=0,
                                        pattern=[[-1, HEADS], [0, P]], channel_multiplier=1).then_inc(consts_made, 1)
            pool.wait_ge(consts_made, 7)
            nc.gpsimd.iota(countdown[:], pattern=[[-1, N]], base=N, channel_multiplier=0,
                           allow_small_or_imprecise_dtypes=True).then_inc(consts_made, 1)
            nc.gpsimd.iota(row_base[:], pattern=[[STRIDE, B]], base=N, channel_multiplier=0,
                           allow_small_or_imprecise_dtypes=True).then_inc(consts_made, 1)
            pool.wait_ge(first_rows_stored, (1 + B) * 16)
            for c in range(LAST + 1):
                pool.sem_inc(near_used[c], 1)

            def gather_part(n, q, c, rows, done):
                pool.wait_ge(near_used[c], n + 1)
                pool.sem_inc(passed, 1)
                for k in PARTS[c]:
                    nc.gpsimd.indirect_dma_start(
                        out=near[:, k, :], out_offset=None, in_=rows,
                        in_offset=bass.IndirectOffsetOnAxis(ap=index[:, q, k:k + 1], axis=0)
                    ).then_inc(done, 16)

            with pool.Fori(0, T // 2) as pair:
                for q in range(2):
                    n = pair * 2 + q
                    pool.wait_ge(index_ready, n + 1)
                    for c in range(LAST):
                        gather_part(n, q, c, hrows[0:STRIDE, :], gathered[c])
                    long = pool.value_load(long_lists[0:1, bass.ds(n, 1)], min_val=0, max_val=1)
                    with pool.If(long > 0):
                        gather_part(n, q, LAST, hrows[0:STRIDE, :], first_gathered)
            pool.wait_ge(other_rows_stored, (B - 1) * 16)
            pool.sem_inc(passed, 1)
            with pool.Fori(T // 2, B * T // 2) as pair:
                for q in range(2):
                    n = pair * 2 + q
                    pool.wait_ge(index_ready, n + 1)
                    for c in range(LAST + 1):
                        gather_part(n, q, c, hrows, gathered[c])

        def wait_tile(eng, b, t, q):
            eng.wait_ge(adj_in_loaded[q], b * (16 * T // 2) + (t - q) * 8 + 16)

        def wait_late_tile(eng, b, i):
            eng.wait_ge(adj_in_loaded[0], (b * (T // 2) + (i + (T - 1)) // 2) * 16)
            eng.wait_ge(adj_in_loaded[1], (b * (T // 2) + (i + (T - 2)) // 2) * 16)

        @block.vector
        def _(dve):
            def norm_stats(xv, ready, made, count, scaled):
                for t in range(T):
                    nc.vector.bn_stats(stats[:, t, :], xv[:, t, :])
                dve.drain()
                for t in range(T):
                    nc.vector.bn_aggr(mean_var[:, t, :], stats[:, t, :])
                dve.drain()
                nc.vector.tensor_scalar(var_eps[:], mean_var[:, :, 1], EPS, None, ALU.add).then_inc(ready, 1)
                dve.wait_ge(made, count)
                nc.vector.reciprocal(rstd[:], std[:])
                dve.drain()
                nc.vector.scalar_tensor_tensor(out=minus_mean[:], in0=mean_var[:, :, 0], scalar=-1.0,
                                               in1=rstd[:], op0=ALU.mult, op1=ALU.mult).then_inc(scaled, 1)

            def first_stats(b):
                if b:
                    dve.wait_ge(other_x_loaded, (B - 1) * 16)
                    dve.wait_ge(first_h, b)
                else:
                    dve.wait_ge(first_x_loaded, 16)
                norm_stats(W[:, b, :].rearrange("p (t f) -> p t f", t=T), first_var, first_std, b + 1, first_scale)

            def list_keys(tile):
                dve.sem_inc(passed, 1)
                row = tile.rearrange("p a n -> p (a n)")
                nc.vector.scalar_tensor_tensor(out=key[:], in0=row, scalar=0.0, in1=countdown[:],
                                               op0=ALU.not_equal, op1=ALU.mult).then_inc(adj_keyed, 1)

            def list_round(r):
                dve.drain()
                nc.vector.max(out=top[:, 8 * r:8 * r + 8], in_=key[:])
                if r < ROUNDS - 1:
                    dve.drain()
                    nc.vector.match_replace(out=key[:], in_to_replace=top[:, 8 * r:8 * r + 8],
                                            in_values=key[:], imm_value=0.0)

            def list_index(b, dst):
                dve.drain()
                nc.vector.tensor_scalar(dst.rearrange("p a n -> p (a n)"), top[:, 0:FIRST], -1.0,
                                        row_base[:, bass.ds(b, 1)], ALU.mult, ALU.add).then_inc(index_ready, 1)

            def neighbour_list(b, t, q):
                wait_tile(dve, b, t, q)
                list_keys(adj_in[:, q:q + 1, :])
                for r in range(ROUNDS):
                    list_round(r)
                list_index(b, index[:, q:q + 1, :])

            def max_part(b, t, c, long_tiles=None):
                row = agg[:, bass.ds(t, 1), :].rearrange("p a f -> p (a f)")
                part = PARTS[c]
                size = len(part) * 16
                dve.drain()
                if long_tiles is not None:
                    dve.wait_ge(first_gathered, long_tiles * size)
                else:
                    dve.wait_ge(gathered[c], (b - (c == LAST)) * (T * size) + t * size + size)
                nc.vector.reduce_max(row if c == 0 else near_max[:],
                                     near[:, part.start:part.stop, :].rearrange("p k f -> p f k"),
                                     AX.X).then_inc(near_used[c], 1)
                if c:
                    dve.drain()
                    combined = nc.vector.tensor_tensor(row, row, near_max[:], ALU.max)
                    if c == LAST:
                        combined.then_inc(agg_ready, 1)

            def neighbour_max(b, t):
                for c in range(LAST + 1):
                    max_part(b, t, c)

            def first_list(t):
                q = t % 2
                wait_tile(dve, 0, t, q)
                list_keys(adj_in[:, q:q + 1, :])
                list_round(0)
                list_round(1)
                dve.drain()
                dve.sem_inc(round_ready, 1)
                dve.wait_ge(long_summed, t + 1)
                nc.vector.tensor_scalar(is_long[:], acc[0:1, t:t + 1], 0.0, None, ALU.is_gt)
                dve.drain()
                nc.vector.tensor_copy(long_lists[0:1, t:t + 1], is_long[:])
                nc.vector.tensor_tensor(long_sum[:], long_sum[:], is_long[:], ALU.add)
                dve.drain()
                nc.vector.tensor_copy(long_sums[0:1, t:t + 1], long_sum[:]).then_inc(long_ready, 1)
                dve.wait_ge(long_ready, t + 1)
                long = dve.value_load(long_lists[0:1, t:t + 1], min_val=0, max_val=1)
                long_tiles = dve.value_load(long_sums[0:1, t:t + 1], min_val=0, max_val=T)
                with dve.If(long > 0):
                    list_round(2)
                    list_round(3)
                with dve.Else():
                    nc.vector.memset(top[:, 16:8 * ROUNDS], 0.0)
                list_index(0, index[:, q:q + 1, :])
                return long, long_tiles

            def first_max(t, long, long_tiles):
                for c in range(LAST):
                    max_part(0, t, c)
                with dve.If(long > 0):
                    max_part(0, t, LAST, long_tiles)
                with dve.Else():
                    dve.drain()
                    dve.sem_inc(near_used[LAST], 1)
                    dve.sem_inc(agg_ready, 1)

            first_stats(0)
            nc.vector.memset(long_sum[:], 0.0)
            dve.wait_ge(consts_made, 9)
            long = first_list(0)
            dve.wait_ge(consts_loaded, LOADS * 16)
            dve.wait_ge(consts_made, 9)
            for col, a_part in ((w1_a[:, 0:1], a1_all[:, 0:D]), (w1_a[:, 1:2], a1_all[:, D:2 * D])):
                nc.vector.tensor_tensor(key[:, 0:D], w1[:], a_part, ALU.mult)
                dve.drain()
                nc.vector.reduce_sum(col, key[:, 0:D], AX.X)
                dve.drain()
            for cols, a_part in ((w2_a[:, 0:HEADS], a2_all[:, 0:HID]),
                                 (w2_a[:, HEADS:2 * HEADS], a2_all[:, HID:2 * HID])):
                prod = key[:, 0:D].rearrange("p (h e) -> p h e", h=HEADS)
                for hd in range(HEADS):
                    nc.vector.tensor_tensor(prod[:, hd, :], w2[:, hd * HID:(hd + 1) * HID], a_part, ALU.mult)
                dve.drain()
                nc.vector.reduce_sum(cols, prod, AX.X)
                dve.drain()
            dve.drain()
            nc.vector.memset(peak[:], 0.0).then_inc(weights_made, 1)
            for t in range(1, T):
                first_stats(t)
                before, long = long, first_list(t)
                first_max(t - 1, *before)
            for b in range(T, B):
                first_stats(b)
            first_max(T - 1, *long)
            dve.wait_ge(other_rows_stored, (B - 1) * 16)

            def normalise(b, layer):
                norm_stats(xg[:], var_ready, std_ready, b * 3 + layer, scale_ready)

            def split_left(b, layer, slope, heads, o_use):
                dve.wait_ge(O_full, b * O_USES + o_use + 1)
                uv = acc[:, 0:2 * T * heads].rearrange("p (t c h) -> p t c h", t=T, c=2)
                u, v = uv[:, :, 0, :], uv[:, :, 1, :]
                nc.vector.tensor_scalar(V[:, :, 0:heads], v, 1.0 - slope, None, ALU.mult).then_inc(v_ready, 1)
                nc.vector.tensor_scalar(su[:, :, 0:heads], u, slope, None, ALU.mult)
                if layer == 2:
                    nc.vector.tensor_copy(many_kinds[:], acc[0:1, HALF:HALF + 1]).then_inc(many_kinds_ready, 1)
                dve.drain()
                dve.sem_inc(O_free, 1)
                src = su
                for part in range(3):
                    dst = parts[:, :, 32 * part:32 * part + heads]
                    last = nc.vector.tensor_copy(dst, src[:, :, 0:heads])
                    if part < 2:
                        dve.drain()
                        nc.vector.tensor_tensor(rest[:, :, 0:heads], src[:, :, 0:heads], dst, ALU.subtract)
                        dve.drain()
                        src = rest
                last.then_inc(parts_ready, 1)

            def score_row(b, n, slot, a_first, b_first):
                full, free, ps, count = ((A_full, A_free, psA, b * A_USES + a_first),
                                         (B_full, B_free, psB, b * B_USES + b_first))[slot % 2]
                dve.wait_ge(row_relu, b * ROWS + n)
                dve.wait_ge(full, count)
                dve.sem_inc(passed, 1)
                col = slot % 8
                nc.vector.tensor_tensor_reduce(out=W[:, slot, :], in0=W[:, slot, :], in1=ps[:], scale=1.0,
                                               scalar=LOWEST, op0=ALU.add, op1=ALU.max,
                                               accum_out=peak[:, col:col + 1]).then_inc(free, 1)

            def shifts(lo):
                nc.vector.tensor_scalar(minus_max[:, lo:lo + 4], peak[:, lo:lo + 4], -1.0, None,
                                        ALU.mult).then_inc(shift_ready, 1)

            def compare_values(ps, at, half):
                nc.vector.tensor_tensor(near_max[:], ps[:, at:at + P], identity[:], ALU.mult)
                dve.drain()
                nc.vector.reduce_sum(squares[:], near_max[:], AX.X)
                dve.drain()
                nc.vector.tensor_tensor(beyond[:, half:half + 1], squares[:], ps[:, at + P:at + P + 1],
                                        ALU.not_equal).then_inc(beyond_ready, 1)

            def graph(b, prep):
                if prep:
                    wait_tile(dve, b + 1, 0, 0)
                    list_keys(adj_in[:, 0:1, :])
                    for r in range(ROUNDS - 1):
                        list_round(r)

                dve.wait_ge(x_loaded, b * 16 + 16)
                dve.wait_ge(O_full, b * O_USES + O_L0 + 1)
                nc.vector.scalar_tensor_tensor(out=flat(xg[:]), in0=acc[:], scalar=0.0, in1=flat(xg[:]),
                                               op0=ALU.max, op1=ALU.add).then_inc(x_updated, 1)
                dve.wait_ge(x_updated, b * 4 + 1)
                dve.sem_inc(O_free, 1)

                normalise(b, 1)
                if prep:
                    list_round(ROUNDS - 1)
                    list_index(b + 1, index[:, 0:1, :])
                    wait_tile(dve, b + 1, 1, 1)
                    list_keys(adj_in[:, 1:2, :])
                    for r in range(2):
                        list_round(r)
                dve.drain()
                dve.wait_ge(C_full, b * C_USES + C_VALUES + 1)
                compare_values(psC, 0, 0)
                dve.drain()
                dve.sem_inc(C_free, 1)
                split_left(b, 1, SLOPE1, 1, O_V1)
                if prep:
                    for r in range(2, ROUNDS):
                        list_round(r)
                    list_index(b + 1, index[:, 1:2, :])
                    max_part(b + 1, 0, 0)
                for g in range(2):
                    for jt in range(4 * g, 4 * g + 4):
                        if jt >= 2:
                            full, count = ((A_full, b * A_USES + A_MASK1 + jt // 2),
                                           (B_full, b * B_USES + B_MASK1 + jt // 2))[jt % 2]
                            dve.wait_ge(full, count)
                        dve.wait_ge(adj_turned_ready, b * T + jt + 1)
                        nc.vector.tensor_scalar(mask_rows[:, jt % 2, :], adj_turned[:, jt, :], 0.0, NEG,
                                                ALU.is_le, ALU.mult).then_inc(masks_ready, 1)
                        if jt >= 4 * g + 1:
                            score_row(b, jt, jt - 1, A_MASK1 + (jt - 1) // 2 + 1, B_MASK1 + (jt - 1) // 2 + 1)
                    if prep and g == 0:
                        max_part(b + 1, 0, 1)
                    jt = 4 * g + 3
                    score_row(b, jt + 1, jt, A_MASK1 + jt // 2 + 1, B_MASK1 + jt // 2 + 1)
                    dve.drain()
                    shifts(4 * g)

                def scale_s1(g):
                    dve.wait_ge(row_probs, b * ROWS + 4 * g + 4)
                    nc.vector.reciprocal(inv_total[:, 4 * g:4 * g + 4], total[:, 4 * g:4 * g + 4])
                    dve.drain()
                    for jt in range(4 * g, 4 * g + 4):
                        last = nc.vector.tensor_scalar(s[:, jt, :], s[:, jt, :], inv_total[:, jt:jt + 1], None,
                                                       ALU.mult)
                    last.then_inc(s_scaled, 1)

                dve.wait_ge(s_ready, b * 2 + 1)
                scale_s1(0)
                for jt in range(T):
                    nc.vector.tensor_scalar(adj_turned[:, jt, :], adj_turned[:, jt, :], 0.0, NEG,
                                            ALU.is_equal, ALU.mult).then_inc(masks_ready, 1)
                scale_s1(1)
                if prep:
                    max_part(b + 1, 0, LAST)
                    neighbour_list(b + 1, 2, 0)
                    neighbour_max(b + 1, 1)
                dve.wait_ge(gelu_ready, b + 1)
                nc.vector.tensor_tensor(flat(xg[:]), gelu_out, flat(xg[:]), ALU.add).then_inc(x_updated, 1)
                dve.wait_ge(x_updated, b * 4 + 2)

                normalise(b, 2)
                if prep:
                    wait_tile(dve, b + 1, 3, 1)
                    list_keys(adj_in[:, 1:2, :])
                    for r in range(ROUNDS - 1):
                        list_round(r)
                dve.drain()
                dve.wait_ge(values_summed, b * T + T)
                dve.sem_inc(passed, 1)
                compare_values(acc, HALF, 1)
                if prep:
                    list_round(ROUNDS - 1)
                    list_index(b + 1, index[:, 1:2, :])
                split_left(b, 2, SLOPE2, HEADS, O_V2)
                if prep:
                    neighbour_max(b + 1, 2)
                    neighbour_list(b + 1, 4, 0)
                dve.wait_ge(s_ready, b * 2 + 2)

                def scale_s(jt, lo):
                    dve.wait_ge(row_probs, b * ROWS + jt * HEADS + (T + lo + QUAD))
                    nc.vector.reciprocal(inv_total[:, lo:lo + 4], total[:, lo:lo + 4])
                    dve.drain()
                    dve.wait_ge(row_used, b * ROWS + jt * HEADS + (T + 8 + lo - QUAD))
                    cols = slice(lo * HID, (lo + 4) * HID)
                    nc.vector.tensor_tensor(
                        s_now[:, cols].rearrange("p (h e) -> p h e", h=4),
                        s[:, bass.ds(jt, 1), cols].rearrange("p a (h e) -> p (a h) e", h=4),
                        inv_total[:, lo:lo + 4].unsqueeze(2).to_broadcast([P, 4, HID]), ALU.mult).then_inc(s_scaled, 1)

                def next_list(i, step):
                    if not prep:
                        return
                    if step <= LAST:
                        max_part(b + 1, i + (T - 5), step)
                    elif step == LAST + 1:
                        wait_late_tile(dve, b + 1, i)
                        list_keys(adj_in[:, bass.ds((i + 1) % 2, 1), :])
                        list_round(0)
                    else:
                        r = step - LAST - 1
                        if r < ROUNDS:
                            list_round(r)
                        if r == ROUNDS - 1:
                            list_index(b + 1, index[:, bass.ds((i + 1) % 2, 1), :])

                def score_group(i, k, in_between):
                    jt, lo = i * 2 + k // 2, k % 2 * QUAD
                    for hd in range(lo, lo + QUAD):
                        score_row(b, jt * HEADS + (T + hd + 1), k % 4 * QUAD + hd % QUAD,
                                  jt * (HEADS // 2) + (A_MASK2 + hd // 2 + 1),
                                  jt * (HEADS // 2) + (B_MASK2 + hd // 2 + 1))
                        if in_between and hd % 2 == 1:
                            next_list(i, (k - 1) * 2 + (hd - lo) // 2)
                    dve.drain()
                    shifts(lo)

                def scale_group(i, k):
                    scale_s(i * 2 + k // 2, k % 2 * QUAD)

                score_group(0, 0, False)
                dve.sem_inc(passed, 1)
                with dve.Fori(0, GROUPS2 // 4 - 1) as i:
                    for k in range(1, 5):
                        score_group(i, k, True)
                        scale_group(i, k - 1)
                i = GROUPS2 // 4 - 1
                for k in range(1, 4):
                    score_group(i, k, False)
                    scale_group(i, k - 1)
                scale_group(i, 3)
                for q, (ps, full, count, free) in enumerate(((psA, A_full, b * A_USES + A_BACK + 1, A_free),
                                                             (psB, B_full, b * B_USES + B_BACK + 1, B_free))):
                    dve.wait_ge(full, count)
                    for hd in range(QUAD):
                        lo = (q * QUAD + hd) * HID
                        xq = xg[:, :, lo:lo + HID]
                        turned = ps[:].rearrange("p (t f) -> p t f", t=T)[:, :, 32 * hd:32 * hd + HID]
                        last = nc.vector.tensor_tensor(xq, turned, xq, ALU.add)
                    dve.drain()
                    dve.sem_inc(free, 1)
                dve.sem_inc(x_updated, 1)

                normalise(b, 3)
                if prep:
                    neighbour_max(b + 1, T - 2)
                dve.wait_ge(hT_ready, b * 4 + 4)

                def scale_left(it, q):
                    dve.wait_ge(B_full, b * B_USES + it * 2 + (B_L3 - 2))
                    for k in range(KINDS):
                        last = nc.vector.tensor_scalar(scaledT[:, q, k, :], hT[:, bass.ds(it * P, P)],
                                                       a3_cols[:, k:k + 1], None, ALU.mult)
                    last.then_inc(left_scaled, 1)

                def select(it, q):
                    nat = adj_nat[:, bass.ds(b % 2, 1), bass.ds(it, 1), :].rearrange("p c a n -> p (c a n)")
                    dve.wait_ge(C_full, b * C_USES + it + (C_L3 - 1))
                    nc.vector.tensor_scalar(mask_row, nat, 1.0, NEG, ALU.not_equal, ALU.mult)
                    for k in range(1, KINDS):
                        nc.vector.tensor_scalar(kind_mask[:, k, :], nat, k + 1.0, None, ALU.is_equal)
                    dve.drain()
                    for k in range(KINDS):
                        full, free, ps = ((A_full, A_free, psA), (B_full, B_free, psB))[k % 2]
                        base = b * (A_USES, B_USES)[k % 2] + it * 2 + ((A_L3, B_L3)[k % 2] + k // 2 + 1)
                        dve.wait_ge(full, base)
                        if k == 0:
                            nc.vector.tensor_tensor(W[:, q, :], ps[:], mask_row, ALU.add).then_inc(free, 1)
                        else:
                            dve.sem_inc(passed, 1)
                            nc.vector.copy_predicated(W[:, q, :], kind_mask[:, k, :], ps[:]).then_inc(free, 1)
                        dve.drain()
                    nc.vector.scalar_tensor_tensor(out=W[:, q, :], in0=W[:, q, :], scalar=SLOPE3, in1=W[:, q, :],
                                                   op0=ALU.mult, op1=ALU.max)
                    dve.drain()
                    nc.vector.reduce_max(peak3[:, q:q + 1], W[:, q, :], AX.X)
                    dve.drain()
                    nc.vector.tensor_scalar(minus_max3[:, q:q + 1], peak3[:, q:q + 1], -1.0, None,
                                            ALU.mult).then_inc(selected, 1)

                def finish_rows(it, q):
                    dve.wait_ge(probs3, b * T + it + 1)
                    nc.vector.reciprocal(inv_total3[:, q:q + 1], total3[:, q:q + 1])
                    dve.drain()
                    dve.wait_ge(O_full, b * O_USES + it + (O_L3 + 1))
                    xt = xg[:, bass.ds(it, 1), :].rearrange("p a f -> p (a f)")
                    nc.vector.scalar_tensor_tensor(out=xt, in0=acc[:, q * HALF:q * HALF + D], scalar=inv_total3[:, q:q + 1],
                                                   in1=xt, op0=ALU.mult, op1=ALU.add).then_inc(O_free, 1)

                def prepare_single(it, half, q):
                    nat = adj_nat[:, bass.ds(b % 2, 1), bass.ds(it, 1), :].rearrange("p c a n -> p (c a n)")
                    full, count = ((A_full, b * A_USES + half + A_L3), (B_full, b * B_USES + half + B_L3))[q]
                    dve.wait_ge(full, count)
                    nc.vector.tensor_scalar(mask_rows[:, q, :], nat, 1.0, NEG, ALU.not_equal, ALU.mult)
                    nc.vector.tensor_scalar(scaledT[:, q, 0, :], hT[:, bass.ds(it * P, P)], a3_cols[:, 0:1], None,
                                            ALU.mult)
                    dve.drain()
                    dve.sem_inc(left_scaled, 1)

                def single_row(it, half, q):
                    full, count, free, ps = ((A_full, b * A_USES + half + (A_L3 + 1), A_free, psA),
                                             (B_full, b * B_USES + half + (B_L3 + 1), B_free, psB))[q]
                    dve.wait_ge(relu3, b * T + it + 1)
                    dve.wait_ge(full, count)
                    dve.sem_inc(passed, 1)
                    nc.vector.tensor_tensor_reduce(out=W[:, q, :], in0=W[:, q, :], in1=ps[:], scale=1.0,
                                                   scalar=LOWEST, op0=ALU.add, op1=ALU.max,
                                                   accum_out=peak3[:, q:q + 1]).then_inc(free, 1)
                    dve.drain()
                    nc.vector.tensor_scalar(minus_max3[:, q:q + 1], peak3[:, q:q + 1], -SLOPE3, None,
                                            ALU.mult).then_inc(selected, 1)

                dve.wait_ge(many_kinds_ready, b + 1)
                dve.sem_inc(passed, 1)
                kinds = dve.value_load(many_kinds[0:1, 0:1], min_val=0, max_val=2 * P)
                with dve.If(kinds == 0):
                    prepare_single(0, 0, 0)
                    prepare_single(1, 0, 1)
                    single_row(0, 0, 0)
                    with dve.Fori(0, T // 2 - 1) as pair:
                        it = pair * 2
                        prepare_single(it + 2, pair + 1, 0)
                        single_row(it + 1, pair, 1)
                        finish_rows(it, 0)
                        prepare_single(it + 3, pair + 1, 1)
                        single_row(it + 2, pair + 1, 0)
                        finish_rows(it + 1, 1)
                    single_row(T - 1, T // 2 - 1, 1)
                    if prep:
                        neighbour_max(b + 1, T - 1)
                    finish_rows(T - 2, 0)
                    finish_rows(T - 1, 1)
                    dve.drain()
                    for count in (A_full, A_free, B_full, B_free):
                        dve.sem_inc(count, 2 * T - T // 2)
                with dve.Else():
                    scale_left(0, 0)
                    scale_left(1, 1)
                    select(0, 0)
                    with dve.Fori(0, T // 2 - 1) as pair:
                        it = pair * 2
                        scale_left(it + 2, 0)
                        select(it + 1, 1)
                        finish_rows(it, 0)
                        scale_left(it + 3, 1)
                        select(it + 2, 0)
                        finish_rows(it + 1, 1)
                    select(T - 1, 1)
                    if prep:
                        neighbour_max(b + 1, T - 1)
                    finish_rows(T - 2, 0)
                    finish_rows(T - 1, 1)
                    dve.drain()
                nc.vector.memset(peak[:, 0:1], 0.0).then_inc(x_updated, 1)

            with dve.Fori(0, B - 1) as b:
                graph(b, True)
            graph(B - 1, False)

        @block.scalar
        def _(act):
            def first_normalise(b):
                act.wait_ge(first_var, b + 1)
                nc.scalar.activation(std[:], var_eps[:], ACT.Sqrt).then_inc(first_std, 1)
                act.wait_ge(first_scale, b + 1)
                for t in range(T):
                    last = nc.scalar.activation(U[:, b, t * D:(t + 1) * D], W[:, b, t * D:(t + 1) * D], ACT.Relu,
                                                bias=minus_mean[:, t:t + 1], scale=rstd[:, t:t + 1])
                last.then_inc(first_h, 1)

            def take_adj(b, t, q):
                wait_tile(act, b, t, q)
                copy_adj(b, t, adj_in[:, q, :])

            def copy_adj(b, t, tile):
                dst = adj_nat[:, bass.ds(b % 2, 1), bass.ds(t, 1), :].rearrange("p c a n -> p (c a n)")
                nc.scalar.copy(dst, tile).then_inc(adj_nat_ready, 1)

            for t in range(T):
                first_normalise(t)
                take_adj(0, t, t % 2)
            for b in range(T, B):
                first_normalise(b)
            act.wait_ge(other_rows_stored, (B - 1) * 16)

            def graph(b, prep):
                def turn(full, count, src, dst, free, ready, ready_count):
                    act.wait_ge(full, count)
                    nc.scalar.copy(dst, src).then_inc(ready, 1)
                    act.wait_ge(ready, ready_count)
                    act.sem_inc(free, 1)

                def turn_adj(jt):
                    ps, full, free, uses = ((psB, B_full, B_free, B_USES), (psC, C_full, C_free, C_USES))[jt % 2]
                    turn(full, b * uses + adj_use(jt) + 1, ps[:], adj_turned[:, jt, :], free,
                         adj_turned_ready, b * T + jt + 1)

                turn_adj(0)
                turn_adj(1)
                turn(A_full, b * A_USES + A_H0 + 1, psA[:], hT[:], A_free, hT_ready, b * 4 + 1)
                turn(B_full, b * B_USES + B_AGG + 1, psB[:], aggT, B_free, aggT_ready, b + 1)
                turn_adj(2)
                turn_adj(3)
                if prep:
                    take_adj(b + 1, 0, 0)

                def normalise(layer, a_use):
                    act.wait_ge(var_ready, b * 3 + layer)
                    nc.scalar.activation(std[:], var_eps[:], ACT.Sqrt).then_inc(std_ready, 1)
                    act.wait_ge(scale_ready, b * 3 + layer)
                    for t in range(T):
                        last = nc.scalar.activation(h[:, t, :], xg[:, t, :], ACT.Relu, bias=minus_mean[:, t:t + 1],
                                                    scale=rstd[:, t:t + 1])
                        if t % (T // 2) == T // 2 - 1:
                            last.then_inc(h_ready, 1)
                    turn(A_full, b * A_USES + a_use + 1, psA[:], hT[:], A_free, hT_ready, b * 4 + layer + 1)

                def relus(slots, slope, u, v_col):
                    for slot in slots:
                        nc.scalar.activation(W[:, slot, :], u(slot), ACT.Relu, bias=v_col(slot),
                                             scale=(1.0 - slope) / slope).then_inc(row_relu, 1)

                def probabilities(group, slots):
                    act.wait_ge(shift_ready, b * GROUPS + group)
                    for slot in slots:
                        col = slot % 8
                        nc.scalar.activation(W[:, slot, :], W[:, slot, :], ACT.Exp, bias=minus_max[:, col:col + 1],
                                             accum_out=total[:, col:col + 1]).then_inc(row_probs, 1)

                def turn_parts(a_use, layer):
                    turn(A_full, b * A_USES + a_use + 1, psA[0:96, 0:HALF].bitcast(BF16), part_rows[:], A_free,
                         part_rows_ready, b * 2 + layer)

                normalise(1, A_H1)
                turn_adj(4)
                turn_adj(5)
                if prep:
                    take_adj(b + 1, 1, 1)
                turn_adj(6)
                turn_adj(7)
                turn_parts(A_PARTS1, 1)
                turn(B_full, b * B_USES + B_U1 + 1, psB[:], U[:, 0, :], B_free, u_ready, b * (1 + HEADS) + 1)
                act.wait_ge(v_ready, b * 2 + 1)
                relus(range(0, T), SLOPE1, lambda q: U[:, 0, :], lambda q: V[:, q, 0:1])
                turn(C_full, b * C_USES + C_S1 + 1, psC[:], flat(s[:]), C_free, s_ready, b * 2 + 1)
                probabilities(1, range(0, 4))
                probabilities(2, range(4, 8))
                if prep:
                    take_adj(b + 1, 2, 0)
                act.wait_ge(O_full, b * O_USES + O_L1 + 1)
                nc.scalar.activation(gelu_out, acc[:], ACT.Gelu).then_inc(gelu_ready, 1)
                act.wait_ge(gelu_ready, b + 1)
                act.sem_inc(O_free, 1)

                normalise(2, A_H2)
                if prep:
                    take_adj(b + 1, 3, 1)
                turn_parts(A_PARTS2, 2)
                for hd in range(HEADS):
                    ps, full, free, count = ((psB, B_full, B_free, b * B_USES + B_U2 + (hd // 2 + 1)),
                                             (psC, C_full, C_free, b * C_USES + C_U2 + (hd // 2 + 1)))[hd % 2]
                    turn(full, count, ps[:], U[:, hd, :], free, u_ready, b * (1 + HEADS) + (hd + 2))
                turn(A_full, b * A_USES + A_S2 + 1, psA[:], flat(s[:]), A_free, s_ready, b * 2 + 2)
                act.wait_ge(v_ready, b * 2 + 2)
                act.sem_inc(passed, 1)
                if prep:
                    take_adj(b + 1, 4, 0)

                def group_slots(k):
                    return range(k % 4 * QUAD, k % 4 * QUAD + QUAD)

                def group_relus(i, k):
                    jt, lo = i * 2 + k // 2, k % 2 * QUAD
                    act.wait_ge(row_used, b * ROWS + jt * HEADS + (lo + QUAD))
                    relus(group_slots(k), SLOPE2, lambda slot: U[:, slot % HEADS, :],
                          lambda slot: V[:, bass.ds(jt, 1), slot % HEADS:slot % HEADS + 1].rearrange("p a e -> p (a e)"))

                group_relus(0, 0)
                act.sem_inc(passed, 1)
                with act.Fori(0, GROUPS2 // 4 - 1) as i:
                    for k in range(4):
                        group_relus(i, k + 1)
                        probabilities(i * 4 + (k + 3), group_slots(k))
                    if prep:
                        wait_late_tile(act, b + 1, i)
                        act.sem_inc(passed, 1)
                        copy_adj(b + 1, i + (T - 3),
                                 adj_in[:, bass.ds((i + 1) % 2, 1), :].rearrange("p a n -> p (a n)"))
                i = GROUPS2 // 4 - 1
                for k in range(4):
                    if k < 3:
                        group_relus(i, k + 1)
                    probabilities(i * 4 + (k + 3), group_slots(k))
                for q, (ps, full, count, free) in enumerate(((acc, O_full, b * O_USES + O_L2 + 1, O_free),
                                                             (psC, C_full, b * C_USES + C_L2 + 1, C_free))):
                    act.wait_ge(full, count)
                    nc.scalar.activation(sums_turned[q], ps[:], ACT.Identity, bias=bias2_cols[:, q:q + 1])\
                        .then_inc(sums_ready, 1)
                    act.wait_ge(sums_ready, b * 2 + q + 1)
                    act.sem_inc(free, 1)

                normalise(3, A_H3)
                def probabilities3(it, q, scale):
                    act.wait_ge(selected, b * T + it + 1)
                    nc.scalar.activation(W[:, q, :], W[:, q, :], ACT.Exp, bias=minus_max3[:, q:q + 1], scale=scale,
                                         accum_out=total3[:, q:q + 1]).then_inc(probs3, 1)

                def turn_probabilities(it, q):
                    act.wait_ge(O_full, b * O_USES + it + (O_L3 - 1))
                    turn(C_full, b * C_USES + it + (C_L3 + 1), psC[:], flat(probsT[q]), C_free, probsT_ready,
                         b * T + it + 1)

                def single_relu(it, half, q):
                    full, count, ps = ((A_full, b * A_USES + half + (A_L3 + 1), psA),
                                       (B_full, b * B_USES + half + (B_L3 + 1), psB))[q]
                    act.wait_ge(full, count)
                    act.wait_ge(C_full, b * C_USES + it + (C_L3 - 1))
                    nc.scalar.activation(W[:, q, :], ps[:], ACT.Relu, scale=(1.0 - SLOPE3) / SLOPE3).then_inc(relu3, 1)

                act.wait_ge(many_kinds_ready, b + 1)
                act.sem_inc(passed, 1)
                kinds = act.value_load(many_kinds[0:1, 0:1], min_val=0, max_val=2 * P)
                with act.If(kinds == 0):
                    single_relu(0, 0, 0)
                    single_relu(1, 0, 1)
                    probabilities3(0, 0, SLOPE3)
                    with act.Fori(0, T // 2 - 1) as pair:
                        it = pair * 2
                        turn_probabilities(it, 0)
                        probabilities3(it + 1, 1, SLOPE3)
                        single_relu(it + 2, pair + 1, 0)
                        turn_probabilities(it + 1, 1)
                        probabilities3(it + 2, 0, SLOPE3)
                        single_relu(it + 3, pair + 1, 1)
                    turn_probabilities(T - 2, 0)
                    probabilities3(T - 1, 1, SLOPE3)
                    turn_probabilities(T - 1, 1)
                with act.Else():
                    act.sem_inc(relu3, T)
                    with act.Fori(0, T // 2) as pair:
                        for q in range(2):
                            probabilities3(pair * 2 + q, q, 1.0)
                            turn_probabilities(pair * 2 + q, q)
                act.wait_ge(x_updated, b * 4 + 4)
                act.sem_inc(passed, 1)
                act.dma_start(out_view[b], xg[:]).then_inc(out_stored, 16)

            with act.Fori(0, B - 1) as b:
                graph(b, True)
            graph(B - 1, False)

        @block.tensor
        def _(pe):
            for free in (A_free, B_free, C_free, O_free):
                pe.sem_inc(free, 1)
            pe.wait_ge(consts_made, 9)
            pe.sem_inc(row_used, 8)

            def mm(dst, lhsT, rhs, start=True, stop=True):
                return nc.tensor.matmul(dst, lhsT, rhs, start=start, stop=stop, skip_group_check=True)

            for t in range(T):
                pe.wait_ge(round_ready, t + 1)
                mm(acc[0:1, t:t + 1], top[:, 15:16], ones[:, 0:1]).then_inc(long_summed, 1)
            pe.wait_ge(weights_made, 1)
            pe.wait_ge(consts_loaded, LOADS * 16)

            def turn_tiles(dst, src, full):
                for t in range(T):
                    last = nc.tensor.transpose(dst[:, t * P:(t + 1) * P], src(t), identity[:])
                last.then_inc(full, 1)

            def start_sums(acc, row):
                for t in range(T):
                    mm(acc[:, t * D:(t + 1) * D], ones[0:1, :], row, t * D % HALF == 0, False)

            def graph(b):
                def turn_adj(jt):
                    ps, full, free, uses = ((psB, B_full, B_free, B_USES), (psC, C_full, C_free, C_USES))[jt % 2]
                    pe.wait_ge(free, b * uses + adj_use(jt) + 1)
                    for it in range(T):
                        tile = adj_nat[:, bass.ds(b % 2, 1), it, jt * P:(jt + 1) * P].rearrange("p c n -> p (c n)")
                        last = mm(ps[:, it * P:(it + 1) * P], tile, identity16[:])
                    last.then_inc(full, 1)

                pe.wait_ge(adj_nat_ready, b * T + T)
                turn_adj(0)
                turn_adj(1)
                pe.wait_ge(h_loaded, b * 16 + 16)
                pe.wait_ge(A_free, b * A_USES + A_H0 + 1)
                turn_tiles(psA, lambda t: h[:, t, :], A_full)
                pe.wait_ge(agg_ready, b * T + T)
                pe.wait_ge(B_free, b * B_USES + B_AGG + 1)
                turn_tiles(psB, lambda t: agg[:, t, :], B_full)
                pe.wait_ge(hT_ready, b * 4 + 1)
                pe.wait_ge(O_free, b * O_USES + O_L0 + 1)
                start_sums(acc, b0_row[:])
                for t in range(T):
                    mm(acc[:, t * D:(t + 1) * D], hT[:, t * P:(t + 1) * P], w0_own[:], False, False)
                pe.wait_ge(aggT_ready, b + 1)
                for t in range(T):
                    last = mm(acc[:, t * D:(t + 1) * D], aggT[:, t * P:(t + 1) * P], w0_agg[:], False, False)
                last.then_inc(O_full, 1)
                turn_adj(2)
                turn_adj(3)

                def turn_h(layer, a_use):
                    pe.wait_ge(A_free, b * A_USES + a_use + 1)
                    for t in range(T):
                        if t % (T // 2) == 0:
                            pe.wait_ge(h_ready, b * 6 + (layer * 2 - 1 + t // (T // 2)))
                        last = nc.tensor.transpose(psA[:, t * P:(t + 1) * P], h[:, t, :], identity[:])
                    last.then_inc(A_full, 1)
                    pe.wait_ge(hT_ready, b * 4 + layer + 1)

                def spread(ps, rep, full):
                    for c in range(2):
                        last = mm(ps[:, c * HALF:(c + 1) * HALF], rep, hT[:, c * HALF:(c + 1) * HALF])
                    last.then_inc(full, 1)

                def split_rows(a_use, layer):
                    pe.wait_ge(parts_ready, b * 2 + layer)
                    pe.wait_ge(A_free, b * A_USES + a_use + 1)
                    dst = psA[0:96, 0:HALF].bitcast(BF16)
                    for t in range(T):
                        last = nc.tensor.transpose(dst[:, t * P:(t + 1) * P], parts[:, t, :], identity16[:])
                    last.then_inc(A_full, 1)
                    pe.wait_ge(part_rows_ready, b * 2 + layer)

                def spread_parts(ps, hd, full):
                    for c in range(2):
                        last = mm(ps[:, c * HALF:(c + 1) * HALF], pick[:, hd, :], part_rows[:, c * HALF:(c + 1) * HALF])
                    last.then_inc(full, 1)

                def masked_left(ps, hd, mask, full):
                    for c in range(2):
                        cols = slice(c * HALF, (c + 1) * HALF)
                        mm(ps[:, cols], pick[:, hd, :], part_rows[:, cols], True, False)
                    for c in range(2):
                        cols = slice(c * HALF, (c + 1) * HALF)
                        last = mm(ps[:, cols], identity16[:], mask(cols), False, True)
                    last.then_inc(full, 1)

                def project(ps, weight, full):
                    n = weight.shape[1]
                    for t in range(T):
                        last = mm(ps[:, t * n:(t + 1) * n], hT[:, t * P:(t + 1) * P], weight)
                    last.then_inc(full, 1)


                def sum_values(ps, at, half):
                    mm(ps[:, at:at + P], ones[0:1, :], zeros[0:1, :], True, False)
                    pe.sem_inc(passed, 1)
                    with pe.Fori(half * T // 2, (half + 1) * T // 2) as jt:
                        for it in range(T):
                            tile = adj_nat[:, bass.ds(b % 2, 1), it, bass.ds(jt * P, P)].rearrange("p c n -> p (c n)")
                            mm(ps[:, at:at + P], tile, tile, False, False)
                            last = mm(ps[:, at + P:at + P + 1], tile, ones16[:], False, False)
                        last.then_inc(values_summed, 1)

                pe.wait_ge(C_free, b * C_USES + C_VALUES + 1)
                sum_values(psC, 0, 0)
                pe.wait_ge(values_summed, b * T + T // 2)
                pe.sem_inc(C_full, 1)
                turn_h(1, A_H1)
                pe.wait_ge(O_free, b * O_USES + O_V1 + 1)
                project(acc, w1_a[:], O_full)
                turn_adj(4)
                turn_adj(5)
                turn_adj(6)
                turn_adj(7)
                split_rows(A_PARTS1, 1)

                def masks1(jt):
                    ps, full, free, count = ((psA, A_full, A_free, b * A_USES + A_MASK1 + (jt // 2 + 1)),
                                             (psB, B_full, B_free, b * B_USES + B_MASK1 + (jt // 2 + 1)))[jt % 2]
                    pe.wait_ge(masks_ready, b * 2 * T + jt + 1)
                    pe.wait_ge(free, count)
                    masked_left(ps, 0, lambda cols: mask_rows[:, jt % 2, cols], full)

                pe.wait_ge(B_free, b * B_USES + B_U1 + 1)
                spread_parts(psB, 0, B_full)
                masks1(0)
                masks1(1)
                pe.wait_ge(C_free, b * C_USES + C_S1 + 1)
                project(psC, w1[:], C_full)
                for jt in range(2, T):
                    masks1(jt)
                pe.wait_ge(O_free, b * O_USES + O_L1 + 1)
                start_sums(acc, zeros[0:1, :])
                for g in range(2):
                    pe.wait_ge(s_scaled, b * GROUPS + (g + 1))
                    for jt in range(4 * g, 4 * g + 4):
                        for it in range(T):
                            last = mm(acc[:, it * D:(it + 1) * D], W[:, jt, it * P:(it + 1) * P], s[:, jt, :],
                                      False, False)
                        last.then_inc(row_used, 1)
                pe.wait_ge(row_used, b * ROWS + T + 8)
                pe.sem_inc(O_full, 1)

                pe.wait_ge(O_free, b * O_USES + O_V2 + 1)
                sum_values(acc, HALF, 1)
                turn_h(2, A_H2)
                pe.wait_ge(beyond_ready, b * 2 + 2)
                for half in range(2):
                    mm(acc[0:1, HALF:HALF + 1], beyond[:, half:half + 1], ones[:, 0:1], half == 0, half == 1)
                project(acc, w2_a[:], O_full)
                split_rows(A_PARTS2, 2)
                for hd in range(HEADS):
                    ps, full, free, count = ((psB, B_full, B_free, b * B_USES + B_U2 + (hd // 2 + 1)),
                                             (psC, C_full, C_free, b * C_USES + C_U2 + (hd // 2 + 1)))[hd % 2]
                    pe.wait_ge(free, count)
                    spread_parts(ps, hd, full)
                pe.wait_ge(A_free, b * A_USES + A_S2 + 1)
                project(psA, w2[:], A_full)
                pe.wait_ge(O_free, b * O_USES + O_L2 + 1)
                start_sums(acc, zeros[0:1, :])
                pe.wait_ge(C_free, b * C_USES + C_L2 + 1)
                start_sums(psC, zeros[0:1, :])
                pe.wait_ge(masks_ready, b * 2 * T + 2 * T)
                pe.sem_inc(passed, 1)

                def masks(i, k, pair):
                    jt, lo = i * 2 + k // 2, k % 2 * QUAD + pair
                    for hd in range(lo, lo + 2):
                        ps, full, free, uses, first = ((psA, A_full, A_free, A_USES, A_MASK2),
                                                       (psB, B_full, B_free, B_USES, B_MASK2))[hd % 2]
                        pe.wait_ge(free, b * uses + jt * (HEADS // 2) + (first + hd // 2 + 1))
                        masked_left(ps, hd, lambda cols: adj_turned[:, bass.ds(jt, 1), cols]
                                    .rearrange("p a n -> p (a n)"), full)

                def sums(i, k, pair):
                    if pair == 0:
                        pe.wait_ge(s_scaled, b * GROUPS + i * 4 + (k + 3))
                    dst = (acc, psC)[k % 2]
                    for q in range(pair, pair + 2):
                        hd = k % 2 * QUAD + q
                        for c in range(2):
                            last = mm(dst[32 * q:32 * q + HID, c * HALF:(c + 1) * HALF],
                                      s_now[:, hd * HID:(hd + 1) * HID],
                                      W[:, k % 4 * QUAD + q, c * HALF:(c + 1) * HALF], False, False)
                        last.then_inc(row_used, 1)

                def masks_and_sums(i, k):
                    for pair in (0, 2):
                        masks(i, k, pair)
                        sums(i, k - 2, pair)

                for k in range(2):
                    for pair in (0, 2):
                        masks(0, k, pair)
                pe.sem_inc(passed, 1)
                with pe.Fori(0, GROUPS2 // 4 - 1) as i:
                    for k in range(2, 6):
                        masks_and_sums(i, k)
                i = GROUPS2 // 4 - 1
                for k in range(2, 4):
                    masks_and_sums(i, k)
                for k in range(2, 4):
                    for pair in (0, 2):
                        sums(i, k, pair)
                pe.wait_ge(row_used, b * ROWS + ROWS + 8)
                pe.sem_inc(O_full, 1)
                pe.sem_inc(C_full, 1)
                for q, (ps, full, free, count) in enumerate(((psA, A_full, A_free, b * A_USES + A_BACK + 1),
                                                             (psB, B_full, B_free, b * B_USES + B_BACK + 1))):
                    pe.wait_ge(sums_ready, b * 2 + q + 1)
                    pe.wait_ge(free, count)
                    turn_tiles(ps, lambda t: sums_turned[q][:, t * P:(t + 1) * P], full)

                turn_h(3, A_H3)

                def scores(it, q):
                    pe.wait_ge(left_scaled, b * T + it + 1)
                    for k in range(KINDS):
                        ps, full, free, uses, first = ((psA, A_full, A_free, A_USES, A_L3),
                                                       (psB, B_full, B_free, B_USES, B_L3))[k % 2]
                        pe.wait_ge(free, b * uses + it * 2 + (first + k // 2 + 1))
                        spread(ps, scaledT[:, q, k, :], full)

                def combine(it, q, meanwhile=None):
                    pe.wait_ge(probs3, b * T + it + 1)
                    pe.wait_ge(C_free, b * C_USES + it + (C_L3 + 1))
                    turn_tiles(psC, lambda t: W[:, q, t * P:(t + 1) * P], C_full)
                    if meanwhile:
                        meanwhile()
                    pe.wait_ge(probsT_ready, b * T + it + 1)
                    pe.wait_ge(O_free, b * O_USES + it + O_L3)
                    for jt in range(T):
                        last = mm(acc[:, q * HALF:q * HALF + D], probsT[q][:, jt, :], h[:, jt, :], jt == 0, jt == T - 1)
                    last.then_inc(O_full, 1)

                def single_scores(it, half, q):
                    ps, full, free, count = ((psA, A_full, A_free, b * A_USES + half + (A_L3 + 1)),
                                             (psB, B_full, B_free, b * B_USES + half + (B_L3 + 1)))[q]
                    pe.wait_ge(left_scaled, b * T + it + 1)
                    pe.wait_ge(free, count)
                    for c in range(2):
                        cols = slice(c * HALF, (c + 1) * HALF)
                        mm(ps[:, cols], scaledT[:, q, 0, :], hT[:, cols], True, False)
                    for c in range(2):
                        cols = slice(c * HALF, (c + 1) * HALF)
                        last = mm(ps[:, cols], identity16[:], mask_rows[:, q, cols], False, True)
                    last.then_inc(full, 1)

                pe.wait_ge(many_kinds_ready, b + 1)
                pe.sem_inc(passed, 1)
                kinds = pe.value_load(many_kinds[0:1, 0:1], min_val=0, max_val=2 * P)
                with pe.If(kinds == 0):
                    single_scores(0, 0, 0)
                    single_scores(1, 0, 1)
                    with pe.Fori(0, T // 2 - 1) as pair:
                        it = pair * 2
                        combine(it, 0, lambda: single_scores(it + 2, pair + 1, 0))
                        combine(it + 1, 1, lambda: single_scores(it + 3, pair + 1, 1))
                    combine(T - 2, 0)
                    combine(T - 1, 1)
                with pe.Else():
                    scores(0, 0)
                    with pe.Fori(0, T // 2 - 1) as pair:
                        it = pair * 2
                        scores(it + 1, 1)
                        combine(it, 0)
                        scores(it + 2, 0)
                        combine(it + 1, 1)
                    scores(T - 1, 1)
                    combine(T - 2, 0)
                    combine(T - 1, 1)

            with pe.Fori(0, B) as b:
                graph(b)


_INS = ['x', 'adj', 'L0_gnn_W', 'L0_gnn_b', 'L1_gnn_W', 'L1_gnn_a', 'L2_gnn_W', 'L2_gnn_a', 'L2_gnn_bias',
        'L3_gnn_a_0', 'L3_gnn_a_1', 'L3_gnn_a_2', 'L3_gnn_a_3']


def kernel(**inputs):
    import numpy as _np
    import concourse.bacc as _bacc
    from concourse.bass_utils import run_bass_kernel_spmd as _run

    nc = _bacc.Bacc("TRN2", target_bir_lowering=False, num_devices=1)
    arrays, args = {}, []
    for name in _INS:
        a = _np.ascontiguousarray(inputs[name])
        arrays[f"in_{name}_dram"] = a
        args.append(nc.dram_tensor(f"in_{name}_dram", a.shape, mybir.dt.from_np(a.dtype), kind="ExternalInput").ap())
    out = nc.dram_tensor("out_0_dram", inputs['x'].shape, F32, kind="ExternalOutput").ap()
    graph_layers(nc, *args[:9], args[9:], out)
    r = _run(nc, [arrays], core_ids=[0])
    return r.results[0]["out_0_dram"]
```
